# Optimizing a Trainium2 kernel written in Bass

```python
import numpy as np
import jax
import jax.numpy as jnp

def _softmax(x, axis=-1):
    return jax.nn.softmax(x, axis=axis)

def _gelu(x):
    return jax.nn.gelu(x, approximate=True)

def _silu(x):
    return jax.nn.silu(x)

def _sigmoid(x):
    return jax.nn.sigmoid(x)

def _layernorm(x, axis=-1, eps=1e-05):
    m = jnp.mean(x, axis=axis, keepdims=True)
    v = jnp.var(x, axis=axis, keepdims=True)
    return (x - m) / jnp.sqrt(v + eps)

def _scatter_add(tgt, idx, src, axis=0):
    return tgt.at[idx].add(src)

def _segment_sum(src, seg, n):
    return jax.ops.segment_sum(src, seg, n)
kernel_name = 'mk_seq_preln_d1_jaxref_r4_1b314d'

def setup_inputs(seed: int=0):
    np.random.seed(seed)
    _w = jnp.asarray

    def _L0_attn_setup():
        import jax, jax.numpy as jnp
        import numpy as np
        N_HEADS = 16
        DIM = 256
        HEAD_DIM = DIM // N_HEADS
        key = jax.random.key(seed)
        k1, k2, k3, k4, k5 = jax.random.split(key, 5)
        x = jax.random.normal(k1, (4, 512, DIM), dtype=jnp.float32)
        s_attn = 1.0 / np.sqrt(DIM)
        W_attn = jax.random.normal(k2, (DIM, 3 * DIM), dtype=jnp.float32) * s_attn
        b_attn = jax.random.normal(k3, (3 * DIM,), dtype=jnp.float32) * 0.02
        W_proj = jax.random.normal(k4, (DIM, DIM), dtype=jnp.float32) * s_attn
        b_proj = jax.random.normal(k5, (DIM,), dtype=jnp.float32) * 0.02
        return {'x': x, 'W_attn': W_attn, 'b_attn': b_attn, 'W_proj': W_proj, 'b_proj': b_proj}
    _L0_attn_in = _L0_attn_setup()

    def _L0_ffn_setup():
        import jax, jax.numpy as jnp
        import numpy as np

        def _bitlinear(x, w_latent):
            scale = jax.lax.stop_gradient(jnp.clip(jnp.mean(jnp.abs(w_latent), axis=1, keepdims=True), 1e-05, None))
            tern = jnp.clip(jnp.round(w_latent / scale), -1.0, 1.0)
            w = w_latent + jax.lax.stop_gradient(tern - w_latent)
            return x @ (w * scale).T
        key = jax.random.key(seed)
        ks = jax.random.split(key, 6)
        dim, hidden, rank = (256, 1024, 16)
        B, S = (4, 1024)
        x = jax.random.normal(ks[0], (B, S, dim), dtype=jnp.float32)
        w_fc = 0.02 * jax.random.normal(ks[1], (hidden, dim), dtype=jnp.float32)
        w_proj = 0.02 * jax.random.normal(ks[2], (dim, hidden), dtype=jnp.float32)
        u = 0.02 * jax.random.normal(ks[3], (hidden, rank), dtype=jnp.float32)
        v = 0.02 * jax.random.normal(ks[4], (rank, dim), dtype=jnp.float32)
        fast_b = jax.random.normal(ks[5], (rank, rank), dtype=jnp.float32)
        gate = jnp.float32(0.05)
        return {'x': x, 'fast_b': fast_b, 'w_fc': w_fc, 'w_proj': w_proj, 'u': u, 'v': v, 'gate': gate}
    _L0_ffn_in = _L0_ffn_setup()
    _d = {'L0_attn_x': _L0_attn_in['x'], 'L0_attn_W_attn': _L0_attn_in['W_attn'], 'L0_attn_b_attn': _L0_attn_in['b_attn'], 'L0_attn_W_proj': _L0_attn_in['W_proj'], 'L0_attn_b_proj': _L0_attn_in['b_proj'], 'L0_ffn_fast_b': _L0_ffn_in['fast_b'], 'L0_ffn_w_fc': _L0_ffn_in['w_fc'], 'L0_ffn_w_proj': _L0_ffn_in['w_proj'], 'L0_ffn_u': _L0_ffn_in['u'], 'L0_ffn_v': _L0_ffn_in['v'], 'L0_ffn_gate': _L0_ffn_in['gate']}
    _x0 = _d['L0_attn_x']
    _d['L0_attn_x'] = jax.random.normal(jax.random.fold_in(jax.random.key(seed), 1), (4, 2048, 256), dtype=_x0.dtype)
    del _x0
    return _d

def reference(L0_attn_x, L0_attn_W_attn, L0_attn_b_attn, L0_attn_W_proj, L0_attn_b_proj, L0_ffn_fast_b, L0_ffn_w_fc, L0_ffn_w_proj, L0_ffn_u, L0_ffn_v, L0_ffn_gate):

    def _L0_attn_ref(x, W_attn, b_attn, W_proj, b_proj):
        import jax, jax.numpy as jnp
        import numpy as np
        N_HEADS = 16
        DIM = 256
        HEAD_DIM = DIM // N_HEADS
        B, S, D = x.shape
        qkv = x @ W_attn + b_attn
        q, k, v = jnp.split(qkv, 3, axis=2)

        def heads(t):
            return t.reshape(B, S, N_HEADS, HEAD_DIM).transpose(0, 2, 1, 3)
        qh, kh, vh = (heads(q), heads(k), heads(v))
        scale = 1.0 / np.sqrt(HEAD_DIM).astype(np.float32)
        scores = jnp.einsum('bhqd,bhkd->bhqk', qh, kh) * scale
        causal = jnp.tril(jnp.ones((S, S), dtype=bool))
        scores = jnp.where(causal, scores, -jnp.inf)
        probs = jax.nn.softmax(scores, axis=-1)
        out = jnp.einsum('bhqk,bhkd->bhqd', probs, vh)
        out = out.transpose(0, 2, 1, 3).reshape(B, S, D)
        return out @ W_proj + b_proj

    def _L0_ffn_ref(x, fast_b, w_fc, w_proj, u, v, gate):
        import jax, jax.numpy as jnp
        import numpy as np

        def _bitlinear(x, w_latent):
            scale = jax.lax.stop_gradient(jnp.clip(jnp.mean(jnp.abs(w_latent), axis=1, keepdims=True), 1e-05, None))
            tern = jnp.clip(jnp.round(w_latent / scale), -1.0, 1.0)
            w = w_latent + jax.lax.stop_gradient(tern - w_latent)
            return x @ (w * scale).T
        h = _bitlinear(x, w_fc) + gate * (x @ v.T @ fast_b.T @ u.T)
        r = jnp.maximum(h, 0.0)
        return _bitlinear(r * r, w_proj)
    x = L0_attn_x
    x = x + _L0_attn_ref(_layernorm(x, axis=-1), L0_attn_W_attn, L0_attn_b_attn, L0_attn_W_proj, L0_attn_b_proj)
    x = x + _L0_ffn_ref(_layernorm(x, axis=-1), L0_ffn_fast_b, L0_ffn_w_fc, L0_ffn_w_proj, L0_ffn_u, L0_ffn_v, L0_ffn_gate)
    return x

_drawn_inputs = setup_inputs


def setup_inputs(seed=0):
    import zlib

    import numpy as np

    out = dict(_drawn_inputs(seed))
    spreads = {}
    factors = {'L0_attn_b_proj': 2.932, 'L0_ffn_fast_b': 8.0, 'L0_ffn_u': 8.0, 'L0_ffn_v': 8.0}
    for name, (base, spread) in spreads.items():
        noise = np.random.default_rng([zlib.crc32(name.encode()), seed]).standard_normal(out[name].shape)
        drawn = base * np.exp(spread * noise) if base else spread * noise
        out[name] = jnp.asarray(drawn.astype(out[name].dtype))
    for name, factor in factors.items():
        out[name] = (out[name] * factor).astype(out[name].dtype)
    return out
```

```python
from contextlib import ExitStack

import concourse.bass as bass
from concourse import mybir

F32 = mybir.dt.float32
BF16 = mybir.dt.bfloat16
ALU = mybir.AluOpType
ACT = mybir.ActivationFunctionType
AX = mybir.AxisListType

P = 128
BATCH, SEQ, DIM = 4, 2048, 256
HEADS = 16
HD = DIM // HEADS
HID = 1024
RANK = 16
SCALE = 0.25
EPS = 1e-5
KD = DIM // P
KH = HID // P
CH = 512
TT = CH // P
NCH = SEQ // CH
GH = 4
GROUPS = HEADS // GH
UNITS = BATCH * GROUPS
KT = SEQ // P
VW = 32
PARTS = 3
TERMS = 6 * HD
MROWS = 2
NEG = -1e30

Q_PART = [0, 1, 2, 0, 1, 0]
K_PART = [0, 0, 0, 1, 1, 2]

STEPS = [(c, j, max(0, j - TT * c) * P) for c in range(NCH) for j in range(TT * (c + 1))]
NS = len(STEPS)
PAIRS = GH // 2
LAG = 6
RING = 4


def max_pieces():
    out = []
    for c in range(NCH):
        for h in range(GH):
            for t in range(TT):
                for i in range(c + 1):
                    out.append((c, h, t, i, CH if i < c else P * (t + 1)))
    return out


PIECES = max_pieces()
PER_STEP = len(PIECES) // NS
NP = len(PIECES)


class Tensors:

    def __init__(self, nc, ctx):
        self.nc, self.ctx = nc, ctx

    def sb(self, name, shape, dt=F32):
        return self.ctx.enter_context(self.nc.sbuf_tensor(name, shape, dt))

    def ps(self, name, shape, dt=F32):
        return self.ctx.enter_context(self.nc.psum_tensor(name, shape, dt))

    def sem(self, name):
        return self.ctx.enter_context(self.nc.semaphore(name))


def build_prep(nc, io, keep):
    with ExitStack() as ctx:
        t = Tensors(nc, ctx)
        fc = t.sb("fc", [P, KH, DIM])
        proj = t.sb("proj", [P, KD, HID])
        fc_a, fc_b = t.sb("fc_a", [P, KH, DIM]), t.sb("fc_b", [P, KH, DIM])
        proj_a, proj_b = t.sb("proj_a", [P, KD, HID]), t.sb("proj_b", [P, KD, HID])
        fc_s, proj_s = t.sb("fc_s", [P, 3, KH]), t.sb("proj_s", [P, 3, KD])
        u_in = t.sb("u_in", [P, KH, RANK])
        u_t = t.sb("u_t", [RANK, HID])
        v_in = t.sb("v_in", [RANK, DIM])
        fast = t.sb("fast", [RANK, RANK])
        fast_t = t.sb("fast_t", [RANK, RANK])
        gate = t.sb("gate", [RANK, 1])
        g_mat = t.sb("g_mat", [RANK, DIM])
        low = t.sb("low", [P, KD, HID])
        ps = t.ps("ps_prep", [P, 8, 512])
        loaded = t.sem("prep_loaded")
        masked = t.sem("prep_masked")
        chain = t.sem("prep_chain")
        done_pe = t.sem("prep_pe")
        done_act = t.sem("prep_act")
        block = ctx.enter_context(nc.Block())

        @block.sync
        def _(sp):
            sp.dma_start(fc[:], io["w_fc"].rearrange("(t p) d -> p t d", p=P)).then_inc(loaded, 16)
            sp.dma_start(proj[:], io["w_proj"].rearrange("(t p) d -> p t d", p=P)).then_inc(loaded, 16)
            sp.dma_start(u_in[:], io["u"].rearrange("(t p) r -> p t r", p=P)).then_inc(loaded, 16)
            sp.dma_start(v_in[:], io["v"]).then_inc(loaded, 16)
            sp.dma_start(fast[:], io["fast_b"]).then_inc(loaded, 16)
            sp.dma_start(gate[:], io["gate"].partition_broadcast(RANK)).then_inc(loaded, 16)
            sp.dma_start(keep["w_qkv"][:], io["W_attn"].rearrange("(k p) n -> p k n", p=P)).then_inc(loaded, 16)
            sp.dma_start(keep["w_o"][:], io["W_proj"].rearrange("(k p) n -> p k n", p=P)).then_inc(loaded, 16)
            sp.dma_start(keep["b_v"][:], io["b_attn"][2 * DIM:3 * DIM].partition_broadcast(P)).then_inc(loaded, 16)
            sp.dma_start(keep["b_o"][:], io["b_proj"].partition_broadcast(P)).then_inc(loaded, 16)
            sp.dma_start(keep["b_qk"][:], io["b_attn"][0:2 * DIM].rearrange("(m p) -> p m", p=P),
                         allow_slow_non_contiguous=True).then_inc(loaded, 16)

        @block.gpsimd
        def _(pool):
            pool.memset(keep["ident"][:], 0.0)
            pool.memset(keep["mask_kq"][:], 0.0)
            pool.memset(keep["mask_qk"][:], 0.0).then_inc(masked, 1)
            pool.wait_ge(masked, 1)
            pool.affine_select(out=keep["ident"][:], in_=keep["ident"][:], compare_op=ALU.not_equal, fill=1.0,
                               base=0, pattern=[[-1, P]], channel_multiplier=1)
            pool.affine_select(out=keep["mask_kq"][:], in_=keep["mask_kq"][:], compare_op=ALU.is_ge, fill=NEG,
                               base=0, pattern=[[1, P]], channel_multiplier=-1)
            diagonal = keep["mask_qk"][:, CH - P:CH]
            pool.affine_select(out=diagonal, in_=diagonal, compare_op=ALU.is_ge, fill=NEG,
                               base=0, pattern=[[-1, P]], channel_multiplier=1).then_inc(masked, 1)
            pool.wait_ge(masked, 2)
            pool.tensor_copy(keep["ident_h"][:], keep["ident"][:])
            pool.tensor_copy(keep["mask_kq_h"][:], keep["mask_kq"][:]).then_inc(masked, 1)

        @block.vector
        def _(dve):
            count = [0]

            def link(ins):
                count[0] += 1
                ins.then_inc(chain, 1)
                dve.wait_ge(chain, count[0])

            dve.wait_ge(loaded, 16 * 11)
            link(dve.tensor_scalar(keep["b_qs"][:], keep["b_qk"][:, 0:KD], SCALE, None, ALU.mult))

            def ternary(w, a, b, s, tiles, width):
                mean, half, minus_half = s[:, 0], s[:, 1], s[:, 2]
                link(dve.tensor_reduce(mean, w[:], AX.X, ALU.add, apply_absolute_value=True))
                link(dve.tensor_scalar(mean, mean, 1.0 / width, 1e-5, ALU.mult, ALU.max))
                dve.tensor_scalar(half, mean, 0.5, None, ALU.mult)
                link(dve.tensor_scalar(minus_half, mean, -0.5, None, ALU.mult))
                for n in range(tiles):
                    dve.tensor_scalar(a[:, n], w[:, n], half[:, n:n + 1], None, ALU.is_gt)
                    last = dve.tensor_scalar(b[:, n], w[:, n], minus_half[:, n:n + 1], None, ALU.is_lt)
                link(last)
                link(dve.tensor_tensor(a[:], a[:], b[:], ALU.subtract))
                link(dve.tensor_tensor(b[:], a[:], w[:], ALU.subtract))
                link(dve.tensor_tensor(a[:], b[:], w[:], ALU.add))
                for n in range(tiles):
                    last = dve.tensor_scalar(a[:, n], a[:, n], mean[:, n:n + 1], None, ALU.mult)
                link(last)

            ternary(fc, fc_a, fc_b, fc_s, KH, DIM)
            ternary(proj, proj_a, proj_b, proj_s, KD, HID)
            dve.wait_ge(done_act, 4)
            for k in range(KD):
                for half in range(2):
                    dve.wait_ge(done_pe, 4 + 2 * k + half)
                    last = dve.tensor_tensor(keep["w1"][:, k, half * 512:half * 512 + 512], ps[:, 4 + 2 * k + half, :],
                                             low[:, k, half * 512:half * 512 + 512], ALU.add)
            last.then_inc(chain, 1)
            count[0] += 1
            dve.wait_ge(done_pe, 8)
            dve.tensor_copy(keep["w2"][:].rearrange("p k d -> p (k d)"),
                            ps[:, 0:4, :].rearrange("p b n -> p (b n)")).then_inc(chain, 1)
            count[0] += 1
            assert count[0] == N_PREP

        @block.scalar
        def _(act):
            act.wait_ge(done_pe, 1)
            act.copy(u_t[:, 0:512], ps[0:RANK, 0, :])
            act.copy(u_t[:, 512:1024], ps[0:RANK, 1, :])
            act.copy(fast_t[:], ps[0:RANK, 2, 0:RANK]).then_inc(done_act, 1)
            act.wait_ge(done_pe, 2)
            act.wait_ge(loaded, 16 * 11)
            act.activation(g_mat[:], ps[0:RANK, 3, 0:DIM], ACT.Copy, scale=gate[:, 0:1]).then_inc(done_act, 1)
            act.wait_ge(done_pe, 3)
            for k in range(KD):
                for half in range(2):
                    last = act.copy(low[:, k, half * 512:half * 512 + 512], ps[:, 4 + 2 * k + half, :])
            last.then_inc(done_act, 2)

        @block.tensor
        def _(pe):
            pe.wait_ge(loaded, 16 * 11)
            pe.wait_ge(masked, 3)
            for n in range(KH):
                pe.transpose(ps[0:RANK, n // 4, (n % 4) * P:(n % 4 + 1) * P], u_in[:, n, :], keep["ident"][:])
            pe.transpose(ps[0:RANK, 2, 0:RANK], fast[:], keep["ident"][0:RANK, 0:RANK]).then_inc(done_pe, 1)
            pe.wait_ge(done_act, 1)
            pe.matmul(ps[0:RANK, 3, 0:DIM], fast_t[:], v_in[:], start=True, stop=True).then_inc(done_pe, 1)
            pe.wait_ge(done_act, 2)
            for k in range(KD):
                for half in range(2):
                    last = pe.matmul(ps[:, 4 + 2 * k + half, :], g_mat[:, k * P:(k + 1) * P],
                                     u_t[:, half * 512:half * 512 + 512], start=True, stop=True)
            last.then_inc(done_pe, 1)
            pe.wait_ge(done_act, 4)
            pe.wait_ge(chain, N_PREP - 2)
            for k in range(KD):
                for half in range(2):
                    for n in range(4):
                        last = pe.transpose(ps[:, 4 + 2 * k + half, n * P:(n + 1) * P],
                                            fc_a[:, 4 * half + n, k * P:(k + 1) * P], keep["ident"][:])
                    last.then_inc(done_pe, 1)
            for n in range(KH):
                for k in range(KD):
                    col = n * DIM + k * P
                    last = pe.transpose(ps[:, col // 512, col % 512:col % 512 + P],
                                        proj_a[:, k, n * P:(n + 1) * P], keep["ident"][:])
            last.then_inc(done_pe, 1)


N_PREP = 1 + 2 * 8 + 2


def wait_apart(eng, sem, value, passed):
    eng.wait_ge(sem, value)
    eng.sem_inc(passed, 1)


class Norm:

    def __init__(self, t, tag):
        self.stats = t.sb(f"stats_{tag}", [P, TT, 6])
        self.mv = t.sb(f"mv_{tag}", [P, TT, 2])
        self.var = t.sb(f"var_{tag}", [P, TT])
        self.root = t.sb(f"root_{tag}", [P, TT])
        self.rstd = t.sb(f"rstd_{tag}", [P, TT])
        self.tmp = t.sb(f"tmp_{tag}", [P, TT])
        self.chain = t.sem(f"norm_chain_{tag}")
        self.rooted = t.sem(f"rooted_{tag}")
        self.passed = t.sem(f"norm_passed_{tag}")

    def normalise(self, dve, x, xn, n):
        base = LN_LINKS * n
        for t in range(TT):
            last = dve.bn_stats(self.stats[:, t], x[:, t])
        last.then_inc(self.chain, 1)
        wait_apart(dve, self.chain, base + 1, self.passed)
        for t in range(TT):
            last = dve.bn_aggr(self.mv[:, t], self.stats[:, t])
        last.then_inc(self.chain, 1)
        dve.wait_ge(self.chain, base + 2)
        dve.tensor_scalar(self.var[:], self.mv[:, :, 1], EPS, None, ALU.add).then_inc(self.chain, 1)
        dve.wait_ge(self.rooted, n + 1)
        dve.reciprocal(self.rstd[:], self.root[:]).then_inc(self.chain, 1)
        dve.wait_ge(self.chain, base + 4)
        dve.tensor_tensor(self.tmp[:], self.rstd[:], self.rstd[:], ALU.mult).then_inc(self.chain, 1)
        dve.wait_ge(self.chain, base + 5)
        dve.tensor_tensor(self.tmp[:], self.tmp[:], self.var[:], ALU.mult).then_inc(self.chain, 1)
        dve.wait_ge(self.chain, base + 6)
        dve.tensor_scalar(self.tmp[:], self.tmp[:], -0.5, 1.5, ALU.mult, ALU.add).then_inc(self.chain, 1)
        dve.wait_ge(self.chain, base + 7)
        dve.tensor_tensor(self.rstd[:], self.rstd[:], self.tmp[:], ALU.mult).then_inc(self.chain, 1)
        dve.wait_ge(self.chain, base + 8)
        for t in range(TT):
            last = dve.tensor_scalar(xn[:, t], x[:, t], self.mv[:, t, 0:1], self.rstd[:, t:t + 1], ALU.subtract, ALU.mult)
        return last

    def take_root(self, act, n):
        act.wait_ge(self.chain, LN_LINKS * n + 3)
        act.activation(self.root[:], self.var[:], ACT.Sqrt).then_inc(self.rooted, 1)


LN_LINKS = 8


STORES = 4 * 2 * PARTS


def build_qkv(nc, io, keep, scr):
    with ExitStack() as ctx:
        t = Tensors(nc, ctx)
        x = [t.sb(f"x{i}", [P, TT, DIM]) for i in range(2)]
        xn = [t.sb(f"xn{i}", [P, TT, DIM]) for i in range(2)]
        xn_t = [t.sb(f"xn_t{i}", [P, KD, CH]) for i in range(2)]
        norm = Norm(t, "attn")
        qk = t.sb("qk", [P, 4, CH])
        rest = t.sb("rest", [P, 4, CH])
        parts = [t.sb(f"parts{i}", [P, 4, PARTS, CH], BF16) for i in range(2)]
        v_out = [t.sb(f"v_out{i}", [P, TT, HEADS, VW]) for i in range(2)]
        ps_t = t.ps("ps_t", [P, 2, 512])
        ps_qk = t.ps("ps_qk", [P, 4, 512])
        ps_v = t.ps("ps_v", [P, 2, 512])
        x_in = [t.sem(f"x_in{i}") for i in range(2)]
        ones_set = t.sem("v_ones_set")
        xn_ready = t.sem("xn_ready")
        xt_ready, xt_copied = t.sem("xt_ready"), t.sem("xt_copied")
        qk_ready, qk_copied = t.sem("qk_ready"), t.sem("qk_copied")
        v_ready, v_copied = t.sem("v_ready"), t.sem("v_copied")
        h_done, rest_done, m_done, l_done = (t.sem(n) for n in ("h_done", "rest_done", "m_done", "l_done"))
        parts_out, v_stored = [t.sem(f"parts_out{i}") for i in range(2)], [t.sem(f"v_stored{i}") for i in range(2)]
        block = ctx.enter_context(nc.Block())
        x_dram = io["x"].rearrange("b (c t p) d -> b c p t d", c=NCH, p=P)
        total = BATCH * NCH

        def over_chunks(eng, body):
            with eng.Fori(0, BATCH - 1) as b:
                for u in range(NCH):
                    body(b, u, NCH * b + u, NCH)
            for u in range(NCH):
                body(BATCH - 1, u, NCH * (BATCH - 1) + u, NCH - 1 - u)

        def used(u, b):
            return 2 * b + u // 2

        @block.sync
        def _(sp):
            def load(b, u, n):
                src = x_dram[bass.ts(b, 1), u].rearrange("o p t d -> (o p) t d")
                sp.dma_start(x[u % 2][:], src).then_inc(x_in[u % 2], 16)

            load(0, 0, 0)
            load(0, 1, 1)

            def body(b, u, n, left):
                if left >= 2:
                    sp.wait_ge(xn_ready, n + 1)
                    load(b + (u + 2) // NCH, (u + 2) % NCH, n + 2)
                for m in range(4):
                    sp.wait_ge(m_done, 4 * n + m + 1)
                    sp.wait_ge(l_done, 4 * n + m + 1)
                    dst = scr["q"] if m < KD else scr["k"]
                    dst = dst.rearrange("(b g) (a d) c (h s) -> b g a c h d s", b=BATCH, d=HD, s=CH)[bass.ts(b, 1)]
                    dst = dst.rearrange("o g a c h d s -> (o g) a c h d s")
                    for g in range(2):
                        for a in range(PARTS):
                            sp.dma_start(dst[2 * (m % KD) + g, a, u], parts[u % 2][g * GH * HD:(g + 1) * GH * HD, m, a, :]
                                         ).then_inc(parts_out[u % 2], 16)

            over_chunks(sp, body)
            for i in range(2):
                sp.wait_ge(parts_out[i], 16 * STORES * total // 2)

        @block.gpsimd
        def _(pool):
            for i in range(2):
                last = pool.memset(v_out[i][:], 1.0)
            last.then_inc(ones_set, 1)

            def body(b, u, n, left):
                for m in range(4):
                    pool.wait_ge(m_done, 4 * n + m + 1)
                    pool.tensor_tensor(parts[u % 2][:, m, 2], rest[:, m], parts[u % 2][:, m, 1],
                                       ALU.subtract).then_inc(l_done, 1)
                pool.wait_ge(v_copied, 2 * n + 2)
                dst = scr["v"].rearrange("(b g) p (c t e) -> b c p t g e", b=BATCH, c=NCH, t=TT)[bass.ts(b, 1), u]
                dst = dst.rearrange("o p t g e -> (o p) t g e")
                src = v_out[u % 2][:].rearrange("p t (g h) e -> p t g (h e)", g=GROUPS)
                for tt in range(TT):
                    pool.dma_start(dst[:, tt], src[:, tt]).then_inc(v_stored[u % 2], 16)

            over_chunks(pool, body)
            for i in range(2):
                pool.wait_ge(v_stored[i], 16 * TT * total // 2)

        @block.vector
        def _(dve):
            def normalise(b, u, n):
                dve.wait_ge(x_in[u % 2], 16 * (used(u, b) + 1))
                if not (isinstance(n, int) and n < 2):
                    dve.wait_ge(xt_ready, KD * (n - 1))
                norm.normalise(dve, x[u % 2], xn[u % 2], n).then_inc(xn_ready, 1)

            normalise(0, 0, 0)
            normalise(0, 1, 1)
            dve.wait_ge(ones_set, 1)

            def body(b, u, n, left):
                if left >= 2:
                    normalise(b + (u + 2) // NCH, (u + 2) % NCH, n + 2)
                dve.wait_ge(parts_out[u % 2], 16 * STORES * used(u, b))
                for m in range(4):
                    dve.wait_ge(qk_copied, 4 * n + m + 1)
                    dve.wait_ge(l_done, 4 * n)
                    dve.tensor_copy(parts[u % 2][:, m, 0], qk[:, m]).then_inc(h_done, 1)
                    dve.wait_ge(h_done, 4 * n + m + 1)
                    dve.tensor_tensor(rest[:, m], qk[:, m], parts[u % 2][:, m, 0], ALU.subtract).then_inc(rest_done, 1)
                    dve.wait_ge(rest_done, 4 * n + m + 1)
                    dve.tensor_copy(parts[u % 2][:, m, 1], rest[:, m]).then_inc(m_done, 1)
                dve.wait_ge(v_stored[u % 2], 16 * TT * used(u, b))
                for i in range(2):
                    dve.wait_ge(v_ready, 2 * n + i + 1)
                    for s in range(2):
                        last = dve.tensor_tensor(
                            v_out[u % 2][:, 2 * i + s, :, 0:HD],
                            ps_v[:, i, s * DIM:(s + 1) * DIM].rearrange("p (h d) -> p h d", d=HD),
                            keep["b_v"][:].rearrange("p (h d) -> p h d", d=HD), ALU.add)
                    last.then_inc(v_copied, 1)

            over_chunks(dve, body)

        @block.scalar
        def _(act):
            def copy_xt(u, n):
                for k in range(KD):
                    act.wait_ge(xt_ready, KD * n + k + 1)
                    act.copy(xn_t[u % 2][:, k], ps_t[:, k]).then_inc(xt_copied, 1)

            norm.take_root(act, 0)
            norm.take_root(act, 1)
            copy_xt(0, 0)

            def body(b, u, n, left):
                if left >= 2:
                    norm.take_root(act, n + 2)
                if left >= 1:
                    copy_xt((u + 1) % NCH, n + 1)
                for m in range(4):
                    act.wait_ge(qk_ready, 4 * n + m + 1)
                    act.wait_ge(rest_done, 4 * n)
                    if m < KD:
                        ins = act.activation(qk[:, m], ps_qk[:, m], ACT.Identity, bias=keep["b_qs"][:, m:m + 1], scale=SCALE)
                    else:
                        ins = act.activation(qk[:, m], ps_qk[:, m], ACT.Identity, bias=keep["b_qk"][:, m:m + 1])
                    ins.then_inc(qk_copied, 1)

            over_chunks(act, body)

        @block.tensor
        def _(pe):
            def transposes(u, n):
                pe.wait_ge(xn_ready, n + 1)
                pe.wait_ge(xt_copied, KD * n)
                for k in range(KD):
                    for tt in range(TT):
                        last = pe.transpose(ps_t[:, k, tt * P:(tt + 1) * P], xn[u % 2][:, tt, k * P:(k + 1) * P], keep["ident"][:])
                    last.then_inc(xt_ready, 1)

            transposes(0, 0)

            def body(b, u, n, left):
                if left >= 1:
                    transposes((u + 1) % NCH, n + 1)
                pe.wait_ge(xt_copied, KD * (n + 1))
                pe.wait_ge(qk_copied, 4 * n)
                for m in range(4):
                    for k in range(KD):
                        last = pe.matmul(ps_qk[:, m], keep["w_qkv"][:, k, m * P:(m + 1) * P], xn_t[u % 2][:, k],
                                         start=(k == 0), stop=(k == KD - 1))
                    last.then_inc(qk_ready, 1)
                pe.wait_ge(v_copied, 2 * n)
                for i in range(2):
                    for s in range(2):
                        tt = 2 * i + s
                        for k in range(KD):
                            last = pe.matmul(ps_v[:, i, s * DIM:(s + 1) * DIM], xn_t[u % 2][:, k, tt * P:(tt + 1) * P],
                                             keep["w_qkv"][:, k, 2 * DIM:3 * DIM], start=(k == 0), stop=(k == KD - 1))
                    last.then_inc(v_ready, 1)

            over_chunks(pe, body)


def build_attention(nc, io, keep, scr):
    with ExitStack() as ctx:
        t = Tensors(nc, ctx)
        qs = [t.sb(f"qs{i}", [TERMS + MROWS, NCH, GH, CH], BF16) for i in range(2)]
        ks = [t.sb(f"ks{i}", [TERMS + MROWS, NCH, GH, CH], BF16) for i in range(2)]
        vs = [t.sb(f"vs{i}", [P, KT, GH, VW]) for i in range(2)]
        probs = t.sb("probs", [P, RING, GH, CH])
        junk = t.sb("junk", [P, 2, CH])
        maxes = t.sb("maxes", [P, GH * TT, NCH])
        neg_max = t.sb("neg_max", [P, GH * TT])
        max_parts = [t.sb(f"max_parts{i}", [P, MROWS, GH * TT], BF16) for i in range(2)]
        max_rows = [t.sb(f"max_rows{i}", [MROWS * GH * TT, P], BF16) for i in range(2)]
        acc_sb = t.sb("acc_sb", [P, CH])
        recip = t.sb("recip", [P, TT, GH, 1])
        out_sb = [t.sb(f"out_sb{i}", [P, TT, GH, HD]) for i in range(2)]
        ps_s = t.ps("ps_s", [P, GH, CH])
        ps_m = t.ps("ps_m", [P, 2, CH])
        ps_acc = t.ps("ps_acc", [P, CH])
        ps_x = t.ps("ps_x", [P, CH])

        ones_set = t.sem("max_ones_set")
        stack_in = [[t.sem(f"stack_in{i}_{half}") for half in range(2)] for i in range(2)]
        v_in = [t.sem(f"v_in{i}") for i in range(2)]
        scores_ready, probs_ready = t.sem("scores_ready"), t.sem("probs_ready")
        pv_done = t.sem("pv_done")
        piece_ready, piece_done, piece_passed = t.sem("piece_ready"), t.sem("piece_done"), t.sem("piece_passed")
        max_chain, max_split = t.sem("max_chain"), t.sem("max_split")
        rows_ready, rows_copied = t.sem("rows_ready"), t.sem("rows_copied")
        rows_in = [t.sem(f"rows_in{i}") for i in range(2)]
        acc_copied, acc_turned = t.sem("acc_copied"), t.sem("acc_turned")
        recip_done, out_ready = t.sem("recip_done"), t.sem("out_ready")
        out_stored = [t.sem(f"out_stored{i}") for i in range(2)]
        block = ctx.enter_context(nc.Block())

        FIRST_END = [NS_OF[c] for c in range(NCH)]

        def rows_at(s):
            g = s - LAG
            return ((FIRST_END.index(g if g > 0 else g + NS), g <= 0) if (g if g > 0 else g + NS) in FIRST_END else None)

        def ended(s, back):
            g = s - back + 1
            g, before = (g, False) if g > 0 else (g + NS, True)
            return (FIRST_END.index(g), before) if g in FIRST_END else None

        def over_units(eng, body):
            body(0, 0, True, False)
            with eng.Fori(0, (UNITS - 2) // 2) as i:
                body(2 * i + 1, 1, False, False)
                body(2 * i + 2, 0, False, False)
            body(UNITS - 1, 1, False, True)

        def pieces_at(s, n, u, last):
            g = s - LAG
            if g < 0:
                unit, par, g = n, u, g + NS
            elif last:
                return []
            else:
                unit, par = n + 1, 1 - u
            return [(unit, par, PER_STEP * g + i, PIECES[PER_STEP * g + i]) for i in range(PER_STEP)]

        def opening(n, u):
            return [(n, u, i, PIECES[i]) for i in range(PER_STEP * (NS - LAG))]

        @block.sync
        def _(sp):
            def load_stack(n, u):
                uses = n // 2
                for half, (a, b) in enumerate(((0, 1), (1, NCH))):
                    for dst, name, repeat in ((qs[u], "q", False), (ks[u], "k", True)):
                        src = scr[name][bass.ts(n, 1)].rearrange("o r c e -> (o r) c e")
                        if repeat:
                            runs = [(0, 0, 1), (1, 0, 1), (2, 0, 1), (3, 1, 1), (4, 1, 1), (5, 2, 1)]
                        else:
                            runs = [(0, 0, 3), (3, 0, 2), (5, 0, 1)]
                        for slot, part, count in runs:
                            sp.dma_start(dst[slot * HD:(slot + count) * HD, a:b].rearrange("r c h s -> r c (h s)"),
                                         src[part * HD:(part + count) * HD, a:b]).then_inc(stack_in[u][half], 16)

            def load_v(n, u):
                src = scr["v"][bass.ts(n, 1)].rearrange("o p e -> (o p) e")
                sp.dma_start(vs[u][:].rearrange("p j h e -> p (j h e)"), src).then_inc(v_in[u], 16)

            def store_rows(n, u, c):
                sp.wait_ge(rows_copied, NCH * n + c + 1)
                for a in range(MROWS):
                    sp.dma_start(ROW_DST(qs[u], a, c), max_rows[c % 2][a * GH * TT:(a + 1) * GH * TT, :]).then_inc(rows_in[c % 2], 16)

            load_stack(0, 0)
            load_v(0, 0)
            for c in range(NCH - 1):
                store_rows(0, 0, c)

            def body(n, u, first, last):
                if not last:
                    if not first:
                        sp.wait_ge(scores_ready, PAIRS * NS * n)
                    load_stack(n + 1, 1 - u)
                    if not first:
                        sp.wait_ge(pv_done, NS * n)
                    load_v(n + 1, 1 - u)
                for s in range(NS):
                    at = rows_at(s)
                    if at and at[1]:
                        store_rows(n, u, at[0])
                    elif at and not last:
                        store_rows(n + 1, 1 - u, at[0])

            over_units(sp, body)

        @block.gpsimd
        def _(pool):
            for i in range(2):
                last = pool.memset(ks[i][TERMS:TERMS + MROWS], 1.0)
            last.then_inc(ones_set, 1)

            def store(n, c):
                pool.wait_ge(out_ready, NCH * n + c + 1)
                dst = scr["o"][bass.ts(n, 1)].rearrange("o (c t p) e -> (o c) p t e", c=NCH, p=P)[c]
                pool.dma_start(dst, out_sb[c % 2][:].rearrange("p t h d -> p t (h d)")).then_inc(out_stored[c % 2], 16)

            def body(n, u, first, last):
                if not first:
                    store(n - 1, NCH - 1)
                for c in range(NCH - 1):
                    store(n, c)
                if last:
                    store(n, NCH - 1)

            over_units(pool, body)
            for i in range(2):
                pool.wait_ge(out_stored[i], 16 * NCH * UNITS // 2)

        @block.scalar
        def _(act):
            def copy_acc(n, c):
                act.wait_ge(pv_done, NS * n + FIRST_END[c])
                act.wait_ge(acc_turned, NCH * n + c)
                act.copy(acc_sb[:], ps_acc[:]).then_inc(acc_copied, 1)

            def body(n, u, first, last):
                for s, (c, j, off) in enumerate(STEPS):
                    if not first or s >= RING:
                        act.wait_ge(pv_done, NS * n + s - RING + 1)
                    for pair in range(PAIRS):
                        act.wait_ge(scores_ready, PAIRS * (NS * n + s) + pair + 1)
                        h = 2 * pair
                        act.activation(probs[:, s % RING, h:h + 2, off:CH], ps_s[:, h:h + 2, off:CH],
                                       ACT.Exp).then_inc(probs_ready, 1)
                    at = ended(s, 1)
                    if at and not (first and at[1]):
                        copy_acc(n - 1 if at[1] else n, at[0])
                if last:
                    copy_acc(n, NCH - 1)

            over_units(act, body)

        @block.vector
        def _(dve):
            def reduce_piece(unit, par, k, piece):
                c, h, tt, i, width = piece
                dst = maxes[:, h * TT + tt, i:i + 1]
                if i < c:
                    dve.wait_ge(piece_ready, NP * unit + k + 1)
                    dve.tensor_reduce(dst, ps_m[:, k % 2, 0:width], AX.X, ALU.max).then_inc(piece_done, 1)
                else:
                    wait_apart(dve, piece_ready, NP * unit + k + 1, piece_passed)
                    dve.tensor_tensor_reduce(out=junk[:, k % 2, 0:width], in0=ps_m[:, k % 2, 0:width],
                                             in1=keep["mask_qk"][:, CH - width:CH], scale=1.0, scalar=NEG,
                                             op0=ALU.add, op1=ALU.max, accum_out=dst).then_inc(piece_done, 1)
                if (h, tt, i) == (GH - 1, TT - 1, c):
                    base = 3 * (NCH * unit + c)
                    dve.wait_ge(piece_done, NP * unit + k + 1)
                    dve.tensor_reduce(neg_max[:], maxes[:, :, 0:c + 1], AX.X, ALU.max, negate=True).then_inc(max_chain, 1)
                    dve.wait_ge(max_chain, base + 1)
                    if not (isinstance(unit, int) and unit == 0 and c < 2):
                        dve.wait_ge(rows_ready, NCH * unit + c - 1)
                    dve.tensor_copy(max_parts[c % 2][:, 0], neg_max[:]).then_inc(max_chain, 1)
                    dve.wait_ge(max_chain, base + 2)
                    dve.tensor_tensor(max_parts[c % 2][:, 1], neg_max[:], max_parts[c % 2][:, 0],
                                      ALU.subtract).then_inc(max_chain, 1)

            def copy_rows(n, c):
                k = NCH * n + c
                dve.wait_ge(rows_ready, k + 1)
                if not (isinstance(n, int) and n == 0 and c < 2):
                    dve.wait_ge(rows_in[c % 2], 16 * MROWS * (2 * n + c // 2))
                dve.tensor_copy(max_rows[c % 2][:], ps_x[0:MROWS * GH * TT, 0:P // 2].bitcast(BF16)).then_inc(rows_copied, 1)

            def normalise(n, c):
                k = NCH * n + c
                dve.wait_ge(acc_turned, k + 1)
                turned = ps_x[:].rearrange("p (t h e) -> p t h e", t=TT, h=GH)
                dve.reciprocal(recip[:], turned[:, :, :, HD:HD + 1]).then_inc(recip_done, 1)
                dve.wait_ge(recip_done, k + 1)
                if not (isinstance(n, int) and n == 0 and c < 2):
                    dve.wait_ge(out_stored[c % 2], 16 * (2 * n + c // 2))
                dve.tensor_tensor(out_sb[c % 2][:], turned[:, :, :, 0:HD], recip[:].to_broadcast([P, TT, GH, HD]),
                                  ALU.mult).then_inc(out_ready, 1)

            pieces = opening(0, 0)
            for s in range(NS - LAG):
                if s in FIRST_END:
                    copy_after = FIRST_END.index(s)
                    for p in pieces[PER_STEP * s:PER_STEP * s + 2]:
                        reduce_piece(*p)
                    copy_rows(0, copy_after)
                    for p in pieces[PER_STEP * s + 2:PER_STEP * (s + 1)]:
                        reduce_piece(*p)
                else:
                    for p in pieces[PER_STEP * s:PER_STEP * (s + 1)]:
                        reduce_piece(*p)

            def body(n, u, first, last):
                for s in range(NS):
                    pieces = pieces_at(s, n, u, last)
                    for p in pieces[:2]:
                        reduce_piece(*p)
                    at = rows_at(s)
                    if at and at[1]:
                        copy_rows(n, at[0])
                    elif at and not last:
                        copy_rows(n + 1, at[0])
                    for p in pieces[2:]:
                        reduce_piece(*p)
                    at = ended(s, 2)
                    if at and not (first and at[1]):
                        normalise(n - 1 if at[1] else n, at[0])
                if last:
                    normalise(n, NCH - 1)

            over_units(dve, body)

        @block.tensor
        def _(pe):
            def form_piece(unit, par, k, piece):
                c, h, tt, i, width = piece
                if not (isinstance(unit, int) and unit == 0 and k < 2):
                    pe.wait_ge(piece_done, NP * unit + k - 1)
                if (h, tt, i) == (0, 0, 0) and c < 2:
                    pe.wait_ge(stack_in[par][c], 16 * 9 * (unit // 2 + 1) if isinstance(unit, int) else STACKS(unit, par))
                pe.matmul(ps_m[:, k % 2, 0:width], qs[par][0:TERMS, c, h, tt * P:(tt + 1) * P],
                          ks[par][0:TERMS, i, h, 0:width], start=True, stop=True).then_inc(piece_ready, 1)

            def turn_rows(n, c, after):
                k = NCH * n + c
                pe.wait_ge(max_chain, 3 * (k + 1))
                if after is not None:
                    pe.wait_ge(out_ready, after)
                pe.transpose(ps_x[0:MROWS * GH * TT, 0:P // 2].bitcast(BF16),
                             max_parts[c % 2][:].rearrange("p a r -> p (a r)"), keep["ident_h"][:]).then_inc(rows_ready, 1)

            def turn_acc(n, c, rows):
                pe.wait_ge(acc_copied, NCH * n + c + 1)
                pe.wait_ge(rows_copied, rows)
                if not (isinstance(n, int) and n == 0 and c == 0):
                    pe.wait_ge(out_ready, NCH * n + c)
                for tt in range(TT):
                    last = pe.transpose(ps_x[:, tt * P:(tt + 1) * P], acc_sb[:, tt * P:(tt + 1) * P], keep["ident"][:])
                last.then_inc(acc_turned, 1)

            def scores(n, u, s, first):
                c, j, off = STEPS[s]
                if j == 0:
                    pe.wait_ge(rows_in[c % 2], 16 * MROWS * (2 * n + c // 2 + 1))
                j0 = j % TT * P
                for h in range(GH):
                    pair = h // 2
                    if h % 2 == 0 and not (first and s == 0):
                        pe.wait_ge(probs_ready, PAIRS * (NS * n + s - 1) + pair + 1)
                    diagonal = j >= TT * c
                    last = pe.matmul(ps_s[:, h, off:CH], ks[u][:, j // TT, h, j0:j0 + P], qs[u][:, c, h, off:CH],
                                     start=True, stop=True)
                    if diagonal:
                        last = pe.matmul(ps_s[:, h, off:off + P], keep["ident_h"][:], keep["mask_kq_h"][:],
                                         start=False, stop=True, skip_group_check=True)
                    if h % 2:
                        last.then_inc(scores_ready, 1)

            def pv(n, u, s):
                c, j, off = STEPS[s]
                if s == 0:
                    pe.wait_ge(v_in[u], 16 * (n // 2 + 1) if isinstance(n, int) else VINS(n, u))
                pe.wait_ge(probs_ready, PAIRS * (NS * n + s + 1))
                if j == 0 and not (isinstance(n, int) and n == 0 and c == 0):
                    pe.wait_ge(acc_copied, NCH * n + c)
                for h in range(GH):
                    last = pe.matmul(ps_acc[h * VW:(h + 1) * VW, off:CH], vs[u][:, j, h], probs[:, s % RING, h, off:CH],
                                     start=(j == 0), stop=(j == TT * (c + 1) - 1), skip_group_check=True)
                last.then_inc(pv_done, 1)

            pe.wait_ge(ones_set, 1)
            pieces = opening(0, 0)
            for s in range(NS - LAG):
                if s in FIRST_END:
                    turn_rows(0, FIRST_END.index(s), None)
                for p in pieces[PER_STEP * s:PER_STEP * (s + 1)]:
                    form_piece(*p)

            def body(n, u, first, last):
                for s in range(NS):
                    scores(n, u, s, first)
                    at = rows_at(s)
                    if at:
                        done = sum(1 for e in FIRST_END if e + 1 < s)
                        after = NCH * n + done
                        if at[1]:
                            turn_rows(n, at[0], after)
                        elif not last:
                            turn_rows(n + 1, at[0], after)
                    pieces = pieces_at(s, n, u, last)
                    for p in pieces[:2]:
                        form_piece(*p)
                    if not (first and s == 0):
                        pv(*((n - 1, 1 - u, NS - 1) if s == 0 else (n, u, s - 1)))
                    for p in pieces[2:]:
                        form_piece(*p)
                    at = ended(s, 2)
                    if at and not (first and at[1]):
                        own = sum(1 for x in range(s + 1) if rows_at(x) and rows_at(x)[1])
                        ahead = 0 if last else sum(1 for x in range(s + 1) if rows_at(x) and not rows_at(x)[1])
                        turn_acc(n - 1 if at[1] else n, at[0], NCH * n + NCH - 1 + own + ahead)
                if last:
                    pv(n, u, NS - 1)
                    turn_acc(n, NCH - 1, NCH * (n + 1))

            over_units(pe, body)


NS_OF = [sum(TT * (i + 1) for i in range(c + 1)) for c in range(NCH)]


def STACKS(unit, par):
    return 8 * 9 * (unit + 2 - par)


def VINS(unit, par):
    return 8 * (unit + 2 - par)


def ROW_DST(stack, a, c):
    return stack[TERMS + a:TERMS + a + 1, c].rearrange("o h (t q) -> o (h t) q", q=P)


def build_mlp(nc, io, keep, scr):
    with ExitStack() as ctx:
        t = Tensors(nc, ctx)
        o_in = [t.sb(f"o_in{i}", [P, TT, GROUPS, GH * HD]) for i in range(2)]
        x = [t.sb(f"mx{i}", [P, TT, DIM]) for i in range(2)]
        x1 = [t.sb(f"x1{i}", [P, TT, DIM]) for i in range(2)]
        xn = t.sb("mxn", [P, TT, DIM])
        o_t = t.sb("o_t", [P, KD, CH])
        xn_t = t.sb("mxn_t", [P, KD, CH])
        norm = Norm(t, "mlp")
        hid = t.sb("hid", [P, KH, CH])
        hid2 = t.sb("hid2", [P, KH, CH])
        y = [t.sb(f"y{i}", [P, TT, DIM]) for i in range(2)]
        ps_h = t.ps("ps_h", [P, 2, CH])
        ps_t = t.ps("mps_t", [P, 2, CH])
        ps_o = t.ps("ps_o", [P, 2, 512])
        ps_y = t.ps("ps_y", [P, 2, 512])
        o_loaded, x_loaded = [t.sem(f"o_loaded{i}") for i in range(2)], [t.sem(f"x_loaded{i}") for i in range(2)]
        xb_done = t.sem("xb_done")
        turned, turned_copied = t.sem("turned"), t.sem("turned_copied")
        o_ready, x1_ready = t.sem("o_ready"), t.sem("x1_ready")
        xn_ready = t.sem("mxn_ready")
        hid_ready, relu_done, square_done = t.sem("hid_ready"), t.sem("relu_done"), t.sem("square_done")
        y_ready, y_done, y_passed = t.sem("y_ready"), t.sem("y_done"), t.sem("y_passed")
        y_stored = [t.sem(f"y_stored{i}") for i in range(2)]
        block = ctx.enter_context(nc.Block())
        x_dram = io["x"].rearrange("b (c t p) d -> b c p t d", c=NCH, p=P)
        y_dram = io["out"].rearrange("b (c t p) d -> b c p t d", c=NCH, p=P)
        o_dram = scr["o"].rearrange("(b g) (c t p) e -> b c p t g e", b=BATCH, c=NCH, p=P)
        total = BATCH * NCH

        def over_chunks(eng, body):
            with eng.Fori(0, BATCH - 1) as b:
                for u in range(NCH):
                    body(b, u, NCH * b + u, NCH)
            for u in range(NCH):
                body(BATCH - 1, u, NCH * (BATCH - 1) + u, NCH - 1 - u)

        def used(u, b):
            return 2 * b + u // 2

        @block.sync
        def _(sp):
            def load(b, u):
                sp.dma_start(x[u % 2][:], x_dram[bass.ts(b, 1), u].rearrange("o p t d -> (o p) t d")).then_inc(x_loaded[u % 2], 16)
                src = o_dram[bass.ts(b, 1), u].rearrange("o p t g e -> (o p) t g e")
                for tt in range(TT):
                    sp.dma_start(o_in[u % 2][:, tt], src[:, tt]).then_inc(o_loaded[u % 2], 16)

            load(0, 0)
            load(0, 1)

            def body(b, u, n, left):
                if left >= 2:
                    sp.wait_ge(x1_ready, 2 * (n + 1))
                    load(b + (u + 2) // NCH, (u + 2) % NCH)
                wait_apart(sp, y_done, 2 * (n + 1), y_passed)
                sp.dma_start(y_dram[bass.ts(b, 1), u].rearrange("o p t d -> (o p) t d"), y[u % 2][:]).then_inc(y_stored[u % 2], 16)

            over_chunks(sp, body)
            for i in range(2):
                sp.wait_ge(y_stored[i], 16 * total // 2)

        @block.gpsimd
        def _(pool):
            def add_bias(b, u, n):
                pool.wait_ge(x_loaded[u % 2], 16 * (used(u, b) + 1))
                for tt in range(TT):
                    last = pool.tensor_tensor(x[u % 2][:, tt], x[u % 2][:, tt], keep["b_o"][:], ALU.add)
                last.then_inc(xb_done, 1)

            def body(b, u, n, left):
                add_bias(b, u, n)

            over_chunks(pool, body)

        @block.vector
        def _(dve):
            def residual_norm(u, n):
                dve.wait_ge(xb_done, n + 1)
                for i in range(2):
                    dve.wait_ge(o_ready, 2 * n + i + 1)
                    dve.tensor_tensor(x1[u % 2][:, 2 * i:2 * i + 2].rearrange("p t d -> p (t d)"), ps_o[:, i],
                                      x[u % 2][:, 2 * i:2 * i + 2].rearrange("p t d -> p (t d)"), ALU.add).then_inc(x1_ready, 1)
                dve.wait_ge(x1_ready, 2 * (n + 1))
                if not (isinstance(n, int) and n == 0):
                    dve.wait_ge(turned, 4 * n)
                norm.normalise(dve, x1[u % 2], xn, n).then_inc(xn_ready, 1)

            residual_norm(0, 0)

            def body(b, u, n, left):
                for m in range(KH):
                    dve.wait_ge(relu_done, KH * n + m + 1)
                    dve.tensor_tensor(hid2[:, m], hid[:, m], hid[:, m], ALU.mult).then_inc(square_done, 1)
                if left >= 1:
                    dve.wait_ge(y_done, 2 * n)
                    residual_norm((u + 1) % NCH, n + 1)
                dve.wait_ge(y_stored[u % 2], 16 * used(u, b))
                for i in range(2):
                    dve.wait_ge(y_ready, 2 * n + i + 1)
                    dve.tensor_tensor(y[u % 2][:, 2 * i:2 * i + 2].rearrange("p t d -> p (t d)"), ps_y[:, i],
                                      x1[u % 2][:, 2 * i:2 * i + 2].rearrange("p t d -> p (t d)"), ALU.add).then_inc(y_done, 1)

            over_chunks(dve, body)

        @block.scalar
        def _(act):
            def copy_turned(dst, first):
                for k in range(KD):
                    act.wait_ge(turned, first + k + 1)
                    act.copy(dst[:, k], ps_t[:, k]).then_inc(turned_copied, 1)

            copy_turned(o_t, 0)
            norm.take_root(act, 0)
            copy_turned(xn_t, 2)

            def body(b, u, n, left):
                for m in range(KH):
                    act.wait_ge(hid_ready, KH * n + m + 1)
                    act.wait_ge(square_done, KH * n)
                    act.activation(hid[:, m], ps_h[:, m % 2], ACT.Relu).then_inc(relu_done, 1)
                if left >= 1:
                    copy_turned(o_t, 4 * (n + 1))
                    norm.take_root(act, n + 1)
                    copy_turned(xn_t, 4 * (n + 1) + 2)

            over_chunks(act, body)

        @block.tensor
        def _(pe):
            def turn(src, first):
                pe.wait_ge(turned_copied, first)
                for k in range(KD):
                    for tt in range(TT):
                        last = pe.transpose(ps_t[:, k, tt * P:(tt + 1) * P], src[:, tt, k * P:(k + 1) * P], keep["ident"][:])
                    last.then_inc(turned, 1)

            def project(b, u, n):
                pe.wait_ge(o_loaded[u % 2], 16 * TT * (used(u, b) + 1))
                turn(o_in[u % 2][:].rearrange("p t g e -> p t (g e)"), 4 * n)
                pe.wait_ge(turned_copied, 4 * n + 2)
                if not (isinstance(n, int) and n == 0):
                    pe.wait_ge(x1_ready, 2 * n)
                for tt in range(TT):
                    for k in range(KD):
                        last = pe.matmul(ps_o[:, tt // 2, (tt % 2) * DIM:(tt % 2 + 1) * DIM], o_t[:, k, tt * P:(tt + 1) * P],
                                         keep["w_o"][:, k], start=(k == 0), stop=(k == KD - 1))
                    if tt % 2:
                        last.then_inc(o_ready, 1)

            def turn_xn(n):
                pe.wait_ge(xn_ready, n + 1)
                turn(xn, 4 * n + 2)

            project(0, 0, 0)
            turn_xn(0)

            def body(b, u, n, left):
                pe.wait_ge(turned_copied, 4 * n + 4)
                for m in range(KH):
                    if m >= 2:
                        pe.wait_ge(relu_done, KH * n + m - 1)
                    for k in range(KD):
                        last = pe.matmul(ps_h[:, m % 2], keep["w1"][:, k, m * P:(m + 1) * P], xn_t[:, k],
                                         start=(k == 0), stop=(k == KD - 1))
                    last.then_inc(hid_ready, 1)
                if left >= 1:
                    project(b + (u + 1) // NCH, (u + 1) % NCH, n + 1)
                pe.wait_ge(square_done, KH * (n + 1))
                if not (isinstance(n, int) and n == 0):
                    pe.wait_ge(y_done, 2 * n)
                for tt in range(TT):
                    for m in range(KH):
                        last = pe.matmul(ps_y[:, tt // 2, (tt % 2) * DIM:(tt % 2 + 1) * DIM], hid2[:, m, tt * P:(tt + 1) * P],
                                         keep["w2"][:, m], start=(m == 0), stop=(m == KH - 1))
                    if tt % 2:
                        last.then_inc(y_ready, 1)
                if left >= 1:
                    turn_xn(n + 1)

            over_chunks(pe, body)


def build_layer(nc, io):
    with ExitStack() as ctx:
        t = Tensors(nc, ctx)
        keep = {
            "w_qkv": t.sb("w_qkv", [P, KD, 3 * DIM]),
            "w_o": t.sb("w_o", [P, KD, DIM]),
            "w1": t.sb("w1", [P, KD, HID]),
            "w2": t.sb("w2", [P, KH, DIM]),
            "b_qk": t.sb("b_qk", [P, 2 * KD]),
            "b_qs": t.sb("b_qs", [P, KD]),
            "b_v": t.sb("b_v", [P, DIM]),
            "b_o": t.sb("b_o", [P, DIM]),
            "ident": t.sb("ident", [P, P]),
            "ident_h": t.sb("ident_h", [P, P], BF16),
            "mask_kq": t.sb("mask_kq", [P, P]),
            "mask_kq_h": t.sb("mask_kq_h", [P, P], BF16),
            "mask_qk": t.sb("mask_qk", [P, CH]),
        }
        scr = {
            "q": nc.dram_tensor("q_scr", [UNITS, PARTS * HD, NCH, GH * CH], BF16).ap(),
            "k": nc.dram_tensor("k_scr", [UNITS, PARTS * HD, NCH, GH * CH], BF16).ap(),
            "v": nc.dram_tensor("v_scr", [UNITS, P, KT * GH * VW], F32).ap(),
            "o": nc.dram_tensor("o_scr", [UNITS, SEQ, GH * HD], F32).ap(),
        }
        build_prep(nc, io, keep)
        build_qkv(nc, io, keep, scr)
        build_attention(nc, io, keep, scr)
        build_mlp(nc, io, keep, scr)


_INS = {
    "L0_attn_x": "x", "L0_attn_W_attn": "W_attn", "L0_attn_b_attn": "b_attn", "L0_attn_W_proj": "W_proj",
    "L0_attn_b_proj": "b_proj", "L0_ffn_fast_b": "fast_b", "L0_ffn_w_fc": "w_fc", "L0_ffn_w_proj": "w_proj",
    "L0_ffn_u": "u", "L0_ffn_v": "v", "L0_ffn_gate": "gate",
}


def kernel(**inputs):
    import numpy as _np
    import concourse.bacc as _bacc
    from concourse import mybir as _mybir
    from concourse.bass_utils import run_bass_kernel_spmd as _run

    nc = _bacc.Bacc("TRN2", target_bir_lowering=False, num_devices=1)
    arrays, io = {}, {}
    for name, short in _INS.items():
        a = _np.ascontiguousarray(inputs[name])
        a = a.reshape(a.shape or (1,))
        arrays[f"in_{name}"] = a
        io[short] = nc.dram_tensor(f"in_{name}", a.shape, _mybir.dt.from_np(a.dtype), kind="ExternalInput").ap()
    io["out"] = nc.dram_tensor("out", (BATCH, SEQ, DIM), F32, kind="ExternalOutput").ap()
    build_layer(nc, io)
    r = _run(nc, [arrays], core_ids=[0])
    return r.results[0]["out"]
```

```python
from contextlib import ExitStack

import concourse.bass as bass
from concourse import mybir

F32 = mybir.dt.float32
F32R = mybir.dt.float32r
BF16 = mybir.dt.bfloat16
ALU = mybir.AluOpType
ACT = mybir.ActivationFunctionType
AX = mybir.AxisListType

P = 128
BATCH, SEQ, DIM = 4, 2048, 256
HEADS = 16
HD = DIM // HEADS
HID = 1024
RANK = 16
SCALE = 0.25
EPS = 1e-5
KD = DIM // P
KH = HID // P
CH = 512
TT = CH // P
NCH = SEQ // CH
GH = 4
GROUPS = HEADS // GH
UNITS = BATCH * GROUPS
KT = SEQ // P
VW = 32
PARTS = 3
TERMS = 6 * HD
MROWS = 2
NEG = -1e30

Q_PART = [0, 1, 2, 0, 1, 0]
K_PART = [0, 0, 0, 1, 1, 2]

STEPS = [(c, j, max(0, j - TT * c) * P) for c in range(NCH) for j in range(TT * (c + 1))]
NS = len(STEPS)
CHUNK_END = [s + 1 for s in range(NS) if s + 1 == NS or STEPS[s + 1][0] > STEPS[s][0]]
DIAGONALS = [s for s, (c, j, off) in enumerate(STEPS) if j >= TT * c]
ND = len(DIAGONALS)
PAIRS = GH // 2
BANKS = 3
ORDER = (0, "piece", 1, 2, "piece", 3, "piece", "pv", "piece")
RING = 4

PIECES = [(c, h, t, i, CH if i < c else P * (t + 1))
          for c in range(NCH) for h in range(GH) for t in range(TT) for i in range(c + 1)]
NP = len(PIECES)
LAG_COLUMNS = 12288
PIECE_PRICE = 96


def schedule():
    ends, at = [], 0
    for c, j, off in STEPS:
        at += GH * (CH - off)
        ends.append(at)
    total, cost = at, sum(piece[4] + PIECE_PRICE for piece in PIECES)
    pieces, at, step_of = [[] for _ in STEPS], LAG_COLUMNS, {}
    for k, piece in enumerate(PIECES):
        ahead = at < total
        step = next(s for s, end in enumerate(ends) if at % total < end)
        pieces[step].append((ahead, k))
        step_of[piece[0]] = (ahead, step)
        at += (piece[4] + PIECE_PRICE) * total // cost
    for at_step in pieces:
        at_step.sort()
    chunks = [[] for _ in STEPS]
    for c, (ahead, step) in step_of.items():
        chunks[(step + 1) % NS].append((ahead and step + 1 < NS, c))
    return pieces, chunks


PIECES_AT, ROWS_AT = schedule()
ROWS_BEFORE = sum(ahead for at in ROWS_AT for ahead, _ in at)


def opening():
    events, waiting = [], []
    ready = [c for at in ROWS_AT for ahead, c in at if ahead]
    for k in sorted(k for at in PIECES_AT for ahead, k in at if ahead):
        events.append(("piece", k))
        for w in waiting:
            w[0] -= 1
        while waiting and waiting[0][0] == 0:
            events.append(tuple(waiting.pop(0)[1:]))
        c = PIECES[k][0]
        if c in ready and (k + 1 == NP or PIECES[k + 1][0] > c):
            waiting += [[4, "turn", c], [8, "copy", c]]
    return events + [tuple(w[1:]) for w in waiting]


def chunk_ended(s, back):
    e = s - back + 1
    before = e <= 0
    e = e + NS if before else e
    return (before, CHUNK_END.index(e)) if e in CHUNK_END else None


def zero(n):
    return isinstance(n, int) and n == 0


def over_chunks(eng, body):
    total = BATCH * NCH
    for n in (0, 1):
        body(n, 0, n, total)
    with eng.Fori(1, total // 2 - 1) as i:
        for u in range(2):
            body(2 * i + u, i, u, total)
    for n in (total - 2, total - 1):
        body(n, n // 2, n % 2, total - 1 - n)


def split_products(pe, out, stationary, moving, start, stop):
    (sh, sl), (mh, ml) = stationary, moving
    pe.matmul(out, sh, mh, start=start, stop=False)
    pe.matmul(out, sh, ml, start=False, stop=False)
    return pe.matmul(out, sl, mh, start=False, stop=stop)


class Tensors:

    def __init__(self, nc, ctx):
        self.nc, self.ctx = nc, ctx

    def sb(self, name, shape, dt=F32):
        return self.ctx.enter_context(self.nc.sbuf_tensor(name, shape, dt))

    def ps(self, name, shape, dt=F32):
        return self.ctx.enter_context(self.nc.psum_tensor(name, shape, dt))

    def sem(self, name):
        return self.ctx.enter_context(self.nc.semaphore(name))


def build_prep(nc, io, keep):
    with ExitStack() as ctx:
        t = Tensors(nc, ctx)
        fc = t.sb("fc", [P, KH, DIM])
        proj = t.sb("proj", [P, KD, HID])
        fc_a, fc_b = t.sb("fc_a", [P, KH, DIM]), t.sb("fc_b", [P, KH, DIM])
        proj_a, proj_b = t.sb("proj_a", [P, KD, HID]), t.sb("proj_b", [P, KD, HID])
        fc_s, proj_s = t.sb("fc_s", [P, 3, KH]), t.sb("proj_s", [P, 3, KD])
        u_in = t.sb("u_in", [P, KH, RANK])
        u_t = t.sb("u_t", [RANK, HID])
        v_in = t.sb("v_in", [RANK, DIM])
        fast = t.sb("fast", [RANK, RANK])
        fast_t = t.sb("fast_t", [RANK, RANK])
        gate = t.sb("gate", [RANK, 1])
        g_mat = t.sb("g_mat", [RANK, DIM])
        low = t.sb("low", [P, KD, HID])
        w1 = t.sb("w1_sum", [P, KD, HID])
        w_qkv, w_o = t.sb("w_qkv_in", [P, KD, 3 * DIM]), t.sb("w_o_in", [P, KD, DIM])
        scale_rows = t.sb("scale_rows", [P, KD, P])
        ps = t.ps("ps_prep", [P, 8, 512])
        loaded, fc_in, proj_in = t.sem("prep_loaded"), t.sem("fc_in"), t.sem("proj_in")
        masked = t.sem("prep_masked")
        chain = t.sem("prep_chain")
        done_pe = t.sem("prep_pe")
        done_act = t.sem("prep_act")
        block = ctx.enter_context(nc.Block())

        @block.sync
        def _(sp):
            sp.dma_start(fc[:], io["w_fc"].rearrange("(t p) d -> p t d", p=P)).then_inc(fc_in, 16)
            sp.dma_start(proj[:], io["w_proj"].rearrange("(t p) d -> p t d", p=P)).then_inc(proj_in, 16)
            sp.dma_start(u_in[:], io["u"].rearrange("(t p) r -> p t r", p=P)).then_inc(loaded, 16)
            sp.dma_start(v_in[:], io["v"]).then_inc(loaded, 16)
            sp.dma_start(fast[:], io["fast_b"]).then_inc(loaded, 16)
            sp.dma_start(gate[:], io["gate"].partition_broadcast(RANK)).then_inc(loaded, 16)
            sp.dma_start(w_qkv[:], io["W_attn"].rearrange("(k p) n -> p k n", p=P)).then_inc(loaded, 16)
            sp.dma_start(w_o[:], io["W_proj"].rearrange("(k p) n -> p k n", p=P)).then_inc(loaded, 16)
            sp.dma_start(keep["b_v"][:], io["b_attn"][2 * DIM:3 * DIM].partition_broadcast(P)).then_inc(loaded, 16)
            sp.dma_start(keep["b_o"][:], io["b_proj"].partition_broadcast(P)).then_inc(loaded, 16)
            sp.dma_start(keep["b_qk"][:], io["b_attn"][0:2 * DIM].rearrange("(m p) -> p m", p=P),
                         allow_slow_non_contiguous=True).then_inc(loaded, 16)

        @block.gpsimd
        def _(pool):
            pool.memset(keep["ident"][:], 0.0)
            pool.memset(keep["mask_qk"][:], 0.0).then_inc(masked, 1)
            pool.wait_ge(masked, 1)
            pool.affine_select(out=keep["ident"][:], in_=keep["ident"][:], compare_op=ALU.not_equal, fill=1.0,
                               base=0, pattern=[[-1, P]], channel_multiplier=1)
            diagonal = keep["mask_qk"][:, CH - P:CH]
            pool.affine_select(out=diagonal, in_=diagonal, compare_op=ALU.is_ge, fill=NEG,
                               base=0, pattern=[[-1, P]], channel_multiplier=1).then_inc(masked, 1)
            pool.wait_ge(masked, 2)
            pool.tensor_copy(keep["ident_h"][:], keep["ident"][:]).then_inc(masked, 1)

        @block.vector
        def _(dve):
            count = [0]

            def link(ins):
                count[0] += 1
                ins.then_inc(chain, 1)
                dve.wait_ge(chain, count[0])

            def split(dst, src):
                link(dve.tensor_copy(dst[:, 0], src))
                dve.tensor_tensor(dst[:, 1], src, dst[:, 0].bitcast(F32), ALU.subtract).then_inc(chain, 1)
                count[0] += 1

            def ternary(w, a, b, s, tiles, width, scaled):
                mean, half, minus_half = s[:, 0], s[:, 1], s[:, 2]
                link(dve.tensor_reduce(mean, w[:], AX.X, ALU.add, apply_absolute_value=True))
                link(dve.tensor_scalar(mean, mean, 1.0 / width, 1e-5, ALU.mult, ALU.max))
                dve.tensor_scalar(half, mean, 0.5, None, ALU.mult)
                link(dve.tensor_scalar(minus_half, mean, -0.5, None, ALU.mult))
                for n in range(tiles):
                    for dst, bound, side in ((a, half, ALU.is_gt), (b, minus_half, ALU.is_lt)):
                        if scaled:
                            last = dve.tensor_scalar(dst[:, n], w[:, n], bound[:, n:n + 1], mean[:, n:n + 1], side, ALU.mult)
                        else:
                            last = dve.tensor_scalar(dst[:, n], w[:, n], bound[:, n:n + 1], None, side)
                link(last)
                link(dve.tensor_tensor(a[:], a[:], b[:], ALU.subtract))

            dve.wait_ge(fc_in, 16)
            ternary(fc, fc_a, fc_b, fc_s, KH, DIM, True)
            dve.wait_ge(proj_in, 16)
            ternary(proj, proj_a, proj_b, proj_s, KD, HID, False)
            for k in range(KD):
                last = dve.tensor_copy(scale_rows[:, k], proj_s[:, 0, k:k + 1].to_broadcast([P, P]))
            link(last)
            dve.wait_ge(loaded, 16 * 9)
            link(dve.tensor_scalar(keep["b_qs"][:], keep["b_qk"][:, 0:KD], SCALE, None, ALU.mult))
            split(keep["w_qkv"], w_qkv[:])
            split(keep["w_o"], w_o[:])
            dve.wait_ge(done_act, 4)
            for k in range(KD):
                for half in range(2):
                    dve.wait_ge(done_pe, 4 + 2 * k + half)
                    last = dve.tensor_tensor(w1[:, k, half * 512:half * 512 + 512], ps[:, 4 + 2 * k + half, :],
                                             low[:, k, half * 512:half * 512 + 512], ALU.add)
            link(last)
            split(keep["w1"], w1[:])
            dve.wait_ge(done_pe, 9)
            dve.tensor_copy(keep["s_out"][:].rearrange("p (k d) -> p k d", d=P),
                            ps[:, 4, 0:DIM].rearrange("p (k d) -> p k d", d=P)).then_inc(chain, 1)
            count[0] += 1
            assert count[0] == N_PREP

        @block.scalar
        def _(act):
            act.wait_ge(done_pe, 1)
            act.copy(u_t[:, 0:512], ps[0:RANK, 0, :])
            act.copy(u_t[:, 512:1024], ps[0:RANK, 1, :])
            act.copy(fast_t[:], ps[0:RANK, 2, 0:RANK]).then_inc(done_act, 1)
            act.wait_ge(done_pe, 2)
            act.wait_ge(loaded, 16 * 9)
            act.activation(g_mat[:], ps[0:RANK, 3, 0:DIM], ACT.Copy, scale=gate[:, 0:1]).then_inc(done_act, 1)
            act.wait_ge(done_pe, 3)
            for k in range(KD):
                for half in range(2):
                    last = act.copy(low[:, k, half * 512:half * 512 + 512], ps[:, 4 + 2 * k + half, :])
            last.then_inc(done_act, 2)
            act.wait_ge(done_pe, 8)
            for b in range(4):
                act.copy(keep["w2"][:, 2 * b:2 * b + 2].rearrange("p k d -> p (k d)"), ps[:, b])

        @block.tensor
        def _(pe):
            pe.wait_ge(loaded, 16 * 9)
            pe.wait_ge(masked, 3)
            for n in range(KH):
                pe.transpose(ps[0:RANK, n // 4, (n % 4) * P:(n % 4 + 1) * P], u_in[:, n, :], keep["ident"][:])
            pe.transpose(ps[0:RANK, 2, 0:RANK], fast[:], keep["ident"][0:RANK, 0:RANK]).then_inc(done_pe, 1)
            pe.wait_ge(done_act, 1)
            pe.matmul(ps[0:RANK, 3, 0:DIM], fast_t[:], v_in[:], start=True, stop=True).then_inc(done_pe, 1)
            pe.wait_ge(done_act, 2)
            for k in range(KD):
                for half in range(2):
                    last = pe.matmul(ps[:, 4 + 2 * k + half, :], g_mat[:, k * P:(k + 1) * P],
                                     u_t[:, half * 512:half * 512 + 512], start=True, stop=True)
            last.then_inc(done_pe, 1)
            pe.wait_ge(done_act, 4)
            pe.wait_ge(chain, N_TERNARY)
            for k in range(KD):
                for half in range(2):
                    for n in range(4):
                        last = pe.transpose(ps[:, 4 + 2 * k + half, n * P:(n + 1) * P],
                                            fc_a[:, 4 * half + n, k * P:(k + 1) * P], keep["ident"][:])
                    last.then_inc(done_pe, 1)
            for n in range(KH):
                for k in range(KD):
                    col = n * DIM + k * P
                    last = pe.transpose(ps[:, col // 512, col % 512:col % 512 + P],
                                        proj_a[:, k, n * P:(n + 1) * P], keep["ident"][:])
            last.then_inc(done_pe, 1)
            pe.wait_ge(chain, N_SUM)
            for k in range(KD):
                last = pe.transpose(ps[:, 4, k * P:(k + 1) * P], scale_rows[:, k], keep["ident"][:])
            last.then_inc(done_pe, 1)


N_TERNARY = 5 + 5 + 1
N_SUM = N_TERNARY + 1 + 4 + 1
N_PREP = N_SUM + 2 + 1


def wait_apart(eng, sem, value, passed):
    eng.wait_ge(sem, value)
    eng.sem_inc(passed, 1)


class Norm:

    def __init__(self, t, tag):
        self.stats = t.sb(f"stats_{tag}", [P, TT, 6])
        self.mv = t.sb(f"mv_{tag}", [P, TT, 2])
        self.var = t.sb(f"var_{tag}", [P, TT])
        self.root = t.sb(f"root_{tag}", [P, TT])
        self.rstd = t.sb(f"rstd_{tag}", [P, TT])
        self.tmp = t.sb(f"tmp_{tag}", [P, TT])
        self.chain = t.sem(f"norm_chain_{tag}")
        self.rooted = t.sem(f"rooted_{tag}")
        self.passed = t.sem(f"norm_passed_{tag}")

    def normalise(self, dve, x, xn, n):
        base = LN_LINKS * n
        for t in range(TT):
            last = dve.bn_stats(self.stats[:, t], x[:, t])
        last.then_inc(self.chain, 1)
        wait_apart(dve, self.chain, base + 1, self.passed)
        for t in range(TT):
            last = dve.bn_aggr(self.mv[:, t], self.stats[:, t])
        last.then_inc(self.chain, 1)
        dve.wait_ge(self.chain, base + 2)
        dve.tensor_scalar(self.var[:], self.mv[:, :, 1], EPS, None, ALU.add).then_inc(self.chain, 1)
        dve.wait_ge(self.rooted, n + 1)
        dve.reciprocal(self.rstd[:], self.root[:]).then_inc(self.chain, 1)
        dve.wait_ge(self.chain, base + 4)
        dve.tensor_tensor(self.tmp[:], self.rstd[:], self.rstd[:], ALU.mult).then_inc(self.chain, 1)
        dve.wait_ge(self.chain, base + 5)
        dve.tensor_tensor(self.tmp[:], self.tmp[:], self.var[:], ALU.mult).then_inc(self.chain, 1)
        dve.wait_ge(self.chain, base + 6)
        dve.tensor_scalar(self.tmp[:], self.tmp[:], -0.5, 1.5, ALU.mult, ALU.add).then_inc(self.chain, 1)
        dve.wait_ge(self.chain, base + 7)
        dve.tensor_tensor(self.rstd[:], self.rstd[:], self.tmp[:], ALU.mult).then_inc(self.chain, 1)
        dve.wait_ge(self.chain, base + 8)
        for t in range(TT):
            last = dve.tensor_scalar(xn[:, t], x[:, t], self.mv[:, t, 0:1], self.rstd[:, t:t + 1], ALU.subtract, ALU.mult)
        return last

    def take_root(self, act, n):
        act.wait_ge(self.chain, LN_LINKS * n + 3)
        act.activation(self.root[:], self.var[:], ACT.Sqrt).then_inc(self.rooted, 1)


LN_LINKS = 8


def copy_high(act, dst, banks, ready, copied, first):
    for k in range(KD):
        act.wait_ge(ready, first + k + 1)
        act.copy(dst[:, 0, k], banks[:, k]).then_inc(copied, 1)


def copy_low(dve, dst, banks, copied, done, first):
    for k in range(KD):
        dve.wait_ge(copied, first + k + 1)
        dve.tensor_tensor(dst[:, 1, k], banks[:, k], dst[:, 0, k].bitcast(F32), ALU.subtract).then_inc(done, 1)


def build_qkv(nc, io, keep, scr):
    with ExitStack() as ctx:
        t = Tensors(nc, ctx)
        x = [t.sb(f"x{i}", [P, TT, DIM]) for i in range(2)]
        xn = [t.sb(f"xn{i}", [P, TT, DIM]) for i in range(2)]
        xn_t = [t.sb(f"xn_t{i}", [P, 2, KD, CH], F32R) for i in range(2)]
        norm = Norm(t, "attn")
        qk = t.sb("qk", [P, 4, CH])
        rest = t.sb("rest", [P, 4, CH])
        parts = [t.sb(f"parts{i}", [P, 4, PARTS, CH], BF16) for i in range(2)]
        v_out = [t.sb(f"v_out{i}", [P, TT, HEADS, VW]) for i in range(2)]
        ps_t = t.ps("ps_t", [P, 2, 512])
        ps_qk = t.ps("ps_qk", [P, 4, 512])
        ps_v = t.ps("ps_v", [P, 2, 512])
        x_in = [t.sem(f"x_in{i}") for i in range(2)]
        ones_set = t.sem("v_ones_set")
        xn_ready = t.sem("xn_ready")
        xt_ready, xt_copied, xt_split = t.sem("xt_ready"), t.sem("xt_copied"), t.sem("xt_split")
        qk_ready, qk_copied = t.sem("qk_ready"), t.sem("qk_copied")
        v_ready, v_copied = t.sem("v_ready"), t.sem("v_copied")
        rest_done, m_done, l_done = (t.sem(n) for n in ("rest_done", "m_done", "l_done"))
        parts_stored, v_stored = [t.sem(f"parts_stored{i}") for i in range(2)], [t.sem(f"v_stored{i}") for i in range(2)]
        block = ctx.enter_context(nc.Block())
        x_dram = io["x"].rearrange("b (c t p) d -> (b c) p t d", c=NCH, p=P)
        uses = BATCH * NCH // 2

        def load(queue, n, u):
            queue.dma_start(x[u][:], x_dram[bass.ts(n, 1)].rearrange("o p t d -> (o p) t d")).then_inc(x_in[u], 16)

        @block.sync
        def _(sp):
            load(sp, 0, 0)
            load(sp, 1, 1)

            def body(n, used, u, left):
                for m in range(4):
                    sp.wait_ge(l_done, 4 * n + m + 1)
                    dst = (scr["q"] if m < KD else scr["k"]).rearrange("b a (f d) (c s) -> b f c d a s", f=KD, s=CH)
                    dst = dst[bass.ts(n // NCH, 1), m % KD, bass.ts(n % NCH, 1)].rearrange("o i d a s -> (o i d) a s")
                    sp.dma_start(dst, parts[u][:, m]).then_inc(parts_stored[u], 16)
                sp.wait_ge(v_copied, 2 * n + 2)
                dst = scr["v"].rearrange("b p (c t) g e -> b c p (t g e)", c=NCH)[bass.ts(n // NCH, 1), bass.ts(n % NCH, 1)]
                sp.dma_start(dst.rearrange("o i p e -> (o i p) e"), v_out[u][:].rearrange("p t h e -> p (t h e)")
                             ).then_inc(v_stored[u], 16)

            over_chunks(sp, body)
            for i in range(2):
                sp.wait_ge(parts_stored[i], 16 * 4 * uses)
                sp.wait_ge(v_stored[i], 16 * uses)

        @block.gpsimd
        def _(pool):
            for i in range(2):
                last = pool.memset(v_out[i][:], 1.0)
            last.then_inc(ones_set, 1)

            def body(n, used, u, left):
                for m in range(4):
                    pool.wait_ge(m_done, 4 * n + m + 1)
                    pool.tensor_tensor(parts[u][:, m, 2], rest[:, m], parts[u][:, m, 1], ALU.subtract).then_inc(l_done, 1)

            over_chunks(pool, body)

        @block.vector
        def _(dve):
            def normalise(n, used, u):
                dve.wait_ge(x_in[u], 16 * (used + 1))
                if not (isinstance(n, int) and n < 2):
                    dve.wait_ge(xt_ready, KD * (n - 1))
                norm.normalise(dve, x[u], xn[u], n).then_inc(xn_ready, 1)

            normalise(0, 0, 0)
            copy_low(dve, xn_t[0], ps_t, xt_copied, xt_split, 0)
            normalise(1, 0, 1)
            dve.wait_ge(ones_set, 1)

            def body(n, used, u, left):
                if left >= 1:
                    copy_low(dve, xn_t[1 - u], ps_t, xt_copied, xt_split, KD * (n + 1))
                if left >= 2:
                    normalise(n + 2, used + 1, u)
                if not zero(used):
                    dve.wait_ge(parts_stored[u], 16 * 4 * used)
                    dve.wait_ge(v_stored[u], 16 * used)
                for m in range(4):
                    dve.wait_ge(qk_copied, 4 * n + m + 1)
                    if not zero(n):
                        dve.wait_ge(l_done, 4 * (n - 1) + m + 1)
                    dve.tensor_tensor(rest[:, m], qk[:, m], parts[u][:, m, 0], ALU.subtract).then_inc(rest_done, 1)
                    dve.wait_ge(rest_done, 4 * n + m + 1)
                    dve.tensor_copy(parts[u][:, m, 1], rest[:, m]).then_inc(m_done, 1)
                for i in range(2):
                    dve.wait_ge(v_ready, 2 * n + i + 1)
                    for s in range(2):
                        last = dve.tensor_tensor(
                            v_out[u][:, 2 * i + s, :, 0:HD],
                            ps_v[:, i, s * DIM:(s + 1) * DIM].rearrange("p (h d) -> p h d", d=HD),
                            keep["b_v"][:].rearrange("p (h d) -> p h d", d=HD), ALU.add)
                    last.then_inc(v_copied, 1)

            over_chunks(dve, body)

        @block.scalar
        def _(act):
            norm.take_root(act, 0)
            copy_high(act, xn_t[0], ps_t, xt_ready, xt_copied, 0)
            norm.take_root(act, 1)

            def body(n, used, u, left):
                if left >= 2:
                    act.wait_ge(xn_ready, n + 1)
                    load(act, n + 2, u)
                if left >= 1:
                    copy_high(act, xn_t[1 - u], ps_t, xt_ready, xt_copied, KD * (n + 1))
                if left >= 2:
                    norm.take_root(act, n + 2)
                for m in range(4):
                    act.wait_ge(qk_ready, 4 * n + m + 1)
                    if not zero(n):
                        act.wait_ge(rest_done, 4 * (n - 1) + m + 1)
                    if m == 0 and not zero(used):
                        act.wait_ge(parts_stored[u], 16 * 4 * used)
                    for dst in (qk[:, m], parts[u][:, m, 0]):
                        if m < KD:
                            ins = act.activation(dst, ps_qk[:, m], ACT.Identity, bias=keep["b_qs"][:, m:m + 1], scale=SCALE)
                        else:
                            ins = act.activation(dst, ps_qk[:, m], ACT.Identity, bias=keep["b_qk"][:, m:m + 1])
                    ins.then_inc(qk_copied, 1)

            over_chunks(act, body)

        @block.tensor
        def _(pe):
            def transposes(n, u):
                pe.wait_ge(xn_ready, n + 1)
                if not zero(n):
                    pe.wait_ge(xt_split, KD * n)
                for k in range(KD):
                    for tt in range(TT):
                        last = pe.transpose(ps_t[:, k, tt * P:(tt + 1) * P], xn[u][:, tt, k * P:(k + 1) * P], keep["ident"][:])
                    last.then_inc(xt_ready, 1)

            transposes(0, 0)

            def body(n, used, u, left):
                if left >= 1:
                    transposes(n + 1, 1 - u)
                pe.wait_ge(xt_split, KD * (n + 1))
                for m in range(4):
                    if not zero(n):
                        pe.wait_ge(qk_copied, 4 * (n - 1) + m + 1)
                    for k in range(KD):
                        last = split_products(pe, ps_qk[:, m], [keep["w_qkv"][:, a, k, m * P:(m + 1) * P] for a in range(2)],
                                              [xn_t[u][:, a, k] for a in range(2)], k == 0, k == KD - 1)
                    last.then_inc(qk_ready, 1)
                for i in range(2):
                    if not zero(n):
                        pe.wait_ge(v_copied, 2 * (n - 1) + i + 1)
                    for s in range(2):
                        tt = 2 * i + s
                        for k in range(KD):
                            last = split_products(pe, ps_v[:, i, s * DIM:(s + 1) * DIM],
                                                  [xn_t[u][:, a, k, tt * P:(tt + 1) * P] for a in range(2)],
                                                  [keep["w_qkv"][:, a, k, 2 * DIM:3 * DIM] for a in range(2)],
                                                  k == 0, k == KD - 1)
                    last.then_inc(v_ready, 1)

            over_chunks(pe, body)


def build_attention(nc, io, keep, scr):
    with ExitStack() as ctx:
        t = Tensors(nc, ctx)
        qs = [t.sb(f"qs{i}", [TERMS + MROWS, NCH, GH, CH], BF16) for i in range(2)]
        ks = [t.sb(f"ks{i}", [TERMS + MROWS, NCH, GH, CH], BF16) for i in range(2)]
        vs = [t.sb(f"vs{i}", [P, KT, GH, VW]) for i in range(2)]
        probs = t.sb("probs", [P, RING, GH, CH])
        junk = t.sb("junk", [P, BANKS, CH])
        maxes = t.sb("maxes", [P, GH * TT, NCH])
        neg_max = t.sb("neg_max", [P, GH * TT])
        max_parts = [t.sb(f"max_parts{i}", [P, MROWS, GH * TT], BF16) for i in range(2)]
        max_rows = [t.sb(f"max_rows{i}", [MROWS * GH * TT, P], BF16) for i in range(2)]
        acc_sb = [t.sb(f"acc_sb{i}", [P, CH]) for i in range(2)]
        recip = [t.sb(f"recip{i}", [P, TT, GH, 1]) for i in range(2)]
        out_sb = [t.sb(f"out_sb{i}", [P, TT, GH, HD]) for i in range(2)]
        ps_s = t.ps("ps_s", [P, BANKS, CH])
        ps_m = t.ps("ps_m", [P, BANKS, CH])
        ps_acc = [t.ps(f"ps_acc{i}", [P, CH]) for i in range(2)]

        ones_set = t.sem("max_ones_set")
        stack_in = [[t.sem(f"stack_in{i}_{c}") for c in range(NCH)] for i in range(2)]
        v_in = [t.sem(f"v_in{i}") for i in range(2)]
        scores_ready = t.sem("scores_ready")
        probs_ready = [t.sem(f"probs_ready{i}") for i in range(2)]
        probs_passed, probs_masked = t.sem("probs_passed"), t.sem("probs_masked")
        pv_done = t.sem("pv_done")
        piece_ready, piece_passed, piece_done = t.sem("piece_ready"), t.sem("piece_passed"), t.sem("piece_done")
        max_chain = t.sem("max_chain")
        rows_turned, rows_copied = t.sem("rows_turned"), t.sem("rows_copied")
        rows_in = [t.sem(f"rows_in{i}") for i in range(2)]
        acc_copied, acc_turned = t.sem("acc_copied"), t.sem("acc_turned")
        recip_done, out_ready = t.sem("recip_done"), t.sem("out_ready")
        out_stored = [t.sem(f"out_stored{i}") for i in range(2)]
        block = ctx.enter_context(nc.Block())

        def over_units(eng, body):
            body(0, 0, True, False)
            with eng.Fori(0, (UNITS - 2) // 2) as i:
                body(2 * i + 1, 1, False, False)
                body(2 * i + 2, 0, False, False)
            body(UNITS - 1, 1, False, True)

        def uses(n, u, by):
            return by * (n // 2 + 1) if isinstance(n, int) else by // 2 * (n + 2 - u)

        def of_step(table, s, n, u, last):
            return [(n + 1, 1 - u, item) if ahead else (n, u, item) for ahead, item in table[s] if not (ahead and last)]

        def shares(items, parts):
            at = [len(items) * i // parts for i in range(parts + 1)]
            return [items[at[i]:at[i + 1]] for i in range(parts)]

        def ended(s, back, n, first):
            at = chunk_ended(s, back)
            return None if at is None or (at[0] and first) else (n - 1 if at[0] else n, at[1])

        def rows_before(s, n, last):
            return NCH * n + ROWS_BEFORE + sum(len(of_step(ROWS_AT, i, n, 0, last)) for i in range(s))

        def accs_before(s, n):
            return NCH * n - 1 + sum(chunk_ended(i, 2) is not None for i in range(s))

        def bank_before(k, total):
            return k - BANKS if k >= BANKS else -1 - (total - 1 - k) % BANKS

        def idle_bank(s):
            return 1 - STEPS[s - 1][0] % 2

        @block.sync
        def _(sp):
            def load_stack(n, u, c):
                for dst, name, slots in ((qs[u], "q", Q_PART), (ks[u], "k", K_PART)):
                    src = scr[name].rearrange("b a (g h d) (c s) -> b g a c d h s", g=GROUPS, d=HD, s=CH)
                    for slot, part in enumerate(slots):
                        from_ = src[bass.ts(n // GROUPS, 1), bass.ts(n % GROUPS, 1), part, c].rearrange("o i d h s -> (o i d) h s")
                        sp.dma_start(dst[slot * HD:(slot + 1) * HD, c], from_).then_inc(stack_in[u][c], 16)

            def load_v(n, u):
                src = scr["v"].rearrange("b p j g e -> b g p j e")[bass.ts(n // GROUPS, 1), bass.ts(n % GROUPS, 1)]
                sp.dma_start(vs[u][:].rearrange("p j h e -> p j (h e)"), src.rearrange("o i p j e -> (o i p) j e")).then_inc(v_in[u], 16)

            def store_rows(n, u, c):
                sp.wait_ge(rows_copied, NCH * n + c + 1)
                for a in range(MROWS):
                    dst = qs[u][TERMS + a:TERMS + a + 1, c].rearrange("o h (t q) -> o (h t) q", q=P)
                    sp.dma_start(dst, max_rows[c % 2][a * GH * TT:(a + 1) * GH * TT, :]).then_inc(rows_in[c % 2], 16)

            def store_out(n, c):
                sp.wait_ge(out_ready, NCH * n + c + 1)
                dst = scr["o"].rearrange("b c p t g e -> b g c p t e")[bass.ts(n // GROUPS, 1), bass.ts(n % GROUPS, 1), c]
                sp.dma_start(dst.rearrange("o i p t e -> (o i p) t e"), out_sb[c % 2][:].rearrange("p t h d -> p t (h d)")
                             ).then_inc(out_stored[c % 2], 16)

            for c in range(NCH):
                load_stack(0, 0, c)
            load_v(0, 0)
            for event, item in opening():
                if event == "copy":
                    store_rows(0, 0, item)

            def body(n, u, first, last):
                if not last:
                    if not first:
                        sp.wait_ge(scores_ready, GH * NS * n)
                    load_stack(n + 1, 1 - u, 0)
                    if not first:
                        sp.wait_ge(pv_done, NS * n)
                    for c in range(1, NCH):
                        load_stack(n + 1, 1 - u, c)
                    load_v(n + 1, 1 - u)
                for s in range(NS):
                    for unit, par, c in of_step(ROWS_AT, s - 1, n, u, last) if s else []:
                        store_rows(unit, par, c)
                    if at := ended(s, 3, n, first):
                        store_out(*at)
                if last:
                    store_out(n, NCH - 1)

            over_units(sp, body)
            for i in range(2):
                sp.wait_ge(out_stored[i], 16 * NCH * UNITS // 2)

        @block.gpsimd
        def _(pool):
            for i in range(2):
                last = pool.memset(ks[i][TERMS:TERMS + MROWS], 1.0)
            last.then_inc(ones_set, 1)

            def body(n, u, first, last):
                heads = PAIRS * NS * n
                for s in DIAGONALS:
                    off = STEPS[s][2]
                    for pair in range(PAIRS):
                        if isinstance(n, int):
                            pool.wait_ge(probs_ready[1], heads + PAIRS * s + pair + 1)
                        else:
                            wait_apart(pool, probs_ready[1], heads + PAIRS * s + pair + 1, probs_passed)
                        tile = probs[:, s % RING, 2 * pair:2 * pair + 2, off:off + P]
                        pool.affine_select(out=tile, in_=tile, compare_op=ALU.is_ge, fill=0.0, base=0,
                                           pattern=[[0, 2], [1, P]], channel_multiplier=-1).then_inc(probs_masked, 1)

            over_units(pool, body)

        @block.scalar
        def _(act):
            def copy_acc(n, c):
                act.wait_ge(pv_done, NS * n + CHUNK_END[c])
                if not (isinstance(n, int) and NCH * n + c < 2):
                    act.wait_ge(acc_turned, NCH * n + c - 1)
                act.copy(acc_sb[c % 2][:], ps_acc[c % 2][:]).then_inc(acc_copied, 1)

            def body(n, u, first, last):
                for s, (c, j, off) in enumerate(STEPS):
                    if not first or s >= RING:
                        act.wait_ge(pv_done, NS * n + s - RING + 1)
                    for h in range(GH):
                        act.wait_ge(scores_ready, GH * NS * n + GH * s + h + 1)
                        act.activation(probs[:, s % RING, h, off:CH], ps_s[:, (GH * s + h) % BANKS, off:CH],
                                       ACT.Exp).then_inc(probs_ready[h % 2], 1)
                    if at := ended(s, 1, n, first):
                        copy_acc(*at)
                if last:
                    copy_acc(n, NCH - 1)

            over_units(act, body)

        @block.vector
        def _(dve):
            def reduce_piece(n, par, k):
                c, h, tt, i, width = PIECES[k]
                dst = maxes[:, h * TT + tt, i:i + 1]
                if i < c:
                    dve.wait_ge(piece_ready, NP * n + k + 1)
                    dve.tensor_reduce(dst, ps_m[:, k % BANKS, 0:width], AX.X, ALU.max).then_inc(piece_done, 1)
                else:
                    if isinstance(n, int):
                        dve.wait_ge(piece_ready, NP * n + k + 1)
                    else:
                        wait_apart(dve, piece_ready, NP * n + k + 1, piece_passed)
                    dve.tensor_tensor_reduce(out=junk[:, k % BANKS, 0:width], in0=ps_m[:, k % BANKS, 0:width],
                                             in1=keep["mask_qk"][:, CH - width:CH], scale=1.0, scalar=NEG,
                                             op0=ALU.add, op1=ALU.max, accum_out=dst).then_inc(piece_done, 1)
                if (h, tt, i) == (GH - 1, TT - 1, c):
                    links = 3 * NCH * n + 3 * c
                    dve.wait_ge(piece_done, NP * n + k + 1)
                    dve.tensor_reduce(neg_max[:], maxes[:, :, 0:c + 1], AX.X, ALU.max, negate=True).then_inc(max_chain, 1)
                    dve.wait_ge(max_chain, links + 1)
                    if not (isinstance(n, int) and NCH * n + c < 2):
                        dve.wait_ge(rows_turned, NCH * n + c - 1)
                    dve.tensor_copy(max_parts[c % 2][:, 0], neg_max[:]).then_inc(max_chain, 1)
                    dve.wait_ge(max_chain, links + 2)
                    dve.tensor_tensor(max_parts[c % 2][:, 1], neg_max[:], max_parts[c % 2][:, 0],
                                      ALU.subtract).then_inc(max_chain, 1)

            def copy_rows(n, c, bank):
                dve.wait_ge(rows_turned, NCH * n + c + 1)
                if not (isinstance(n, int) and NCH * n + c < 2):
                    dve.wait_ge(rows_in[c % 2], 16 * MROWS * 2 * n + 16 * MROWS * (c // 2))
                dve.tensor_copy(max_rows[c % 2][:], ps_acc[bank][0:MROWS * GH * TT, 0:P // 2].bitcast(BF16)).then_inc(rows_copied, 1)

            def normalise(n, c):
                dve.wait_ge(acc_turned, NCH * n + c + 1)
                turned = ps_acc[c % 2][:].rearrange("p (t h e) -> p t h e", t=TT, h=GH)
                dve.reciprocal(recip[c % 2][:], turned[:, :, :, HD:HD + 1]).then_inc(recip_done, 1)
                dve.wait_ge(recip_done, NCH * n + c + 1)
                if not (isinstance(n, int) and NCH * n + c < 2):
                    dve.wait_ge(out_stored[c % 2], 16 * 2 * n + 16 * (c // 2))
                dve.tensor_tensor(out_sb[c % 2][:], turned[:, :, :, 0:HD], recip[c % 2][:].to_broadcast([P, TT, GH, HD]),
                                  ALU.mult).then_inc(out_ready, 1)

            for event, item in opening():
                if event == "piece":
                    reduce_piece(0, 0, item)
                elif event == "copy":
                    copy_rows(0, item, 1)

            def body(n, u, first, last):
                for s in range(NS):
                    one, two = shares(of_step(PIECES_AT, s, n, u, last), 2)
                    for piece in one:
                        reduce_piece(*piece)
                    for unit, par, c in of_step(ROWS_AT, s - 1, n, u, last) if s else []:
                        copy_rows(unit, c, idle_bank(s - 1))
                    if at := ended(s, 3, n, first):
                        normalise(*at)
                    for piece in two:
                        reduce_piece(*piece)
                if last:
                    normalise(n, NCH - 1)

            over_units(dve, body)

        @block.tensor
        def _(pe):
            def form_piece(n, par, k):
                c, h, tt, i, width = PIECES[k]
                if not (zero(n) and k < BANKS):
                    pe.wait_ge(piece_done, NP * n + bank_before(k, NP) + 1)
                if (h, tt, i) == (0, 0, 0):
                    pe.wait_ge(stack_in[par][c], uses(n, par, 16 * len(Q_PART + K_PART)))
                pe.matmul(ps_m[:, k % BANKS, 0:width], qs[par][0:TERMS, c, h, tt * P:(tt + 1) * P],
                          ks[par][0:TERMS, i, h, 0:width], start=True, stop=True).then_inc(piece_ready, 1)

            def turn_rows(n, c, bank, accs):
                pe.wait_ge(max_chain, 3 * NCH * n + 3 * (c + 1))
                if not isinstance(accs, int) or accs > 0:
                    pe.wait_ge(out_ready, accs)
                pe.transpose(ps_acc[bank][0:MROWS * GH * TT, 0:P // 2].bitcast(BF16),
                             max_parts[c % 2][:].rearrange("p a r -> p (a r)"), keep["ident_h"][:]).then_inc(rows_turned, 1)

            def turn_acc(n, c):
                pe.wait_ge(acc_copied, NCH * n + c + 1)
                for tt in range(TT):
                    last = pe.transpose(ps_acc[c % 2][:, tt * P:(tt + 1) * P], acc_sb[c % 2][:, tt * P:(tt + 1) * P], keep["ident"][:])
                last.then_inc(acc_turned, 1)

            def scores(n, u, s, h, first):
                c, j, off = STEPS[s]
                if j == 0 and h == 0:
                    pe.wait_ge(rows_in[c % 2], 16 * MROWS * 2 * n + 16 * MROWS * (c // 2 + 1))
                j0 = j % TT * P
                k = GH * s + h
                if not (first and k < BANKS):
                    before = bank_before(k, GH * NS)
                    pe.wait_ge(probs_ready[before % 2], PAIRS * NS * n + before // 2 + 1)
                pe.matmul(ps_s[:, k % BANKS, off:CH], ks[u][:, j // TT, h, j0:j0 + P], qs[u][:, c, h, off:CH],
                          start=True, stop=True).then_inc(scores_ready, 1)

            def pv(n, u, s, rows, accs):
                c, j, off = STEPS[s]
                if s == 0:
                    pe.wait_ge(v_in[u], uses(n, u, 16))
                if s in DIAGONALS:
                    pe.wait_ge(probs_masked, PAIRS * ND * n + PAIRS * (DIAGONALS.index(s) + 1))
                else:
                    pe.wait_ge(probs_ready[1], PAIRS * NS * n + PAIRS * (s + 1))
                if j == 0:
                    pe.wait_ge(rows_copied, rows)
                    if not isinstance(accs, int) or accs > 0:
                        pe.wait_ge(out_ready, accs)
                for h in range(GH):
                    last = pe.matmul(ps_acc[c % 2][h * VW:(h + 1) * VW, off:CH], vs[u][:, j, h], probs[:, s % RING, h, off:CH],
                                     start=(j == 0), stop=(j == TT * (c + 1) - 1), skip_group_check=True)
                last.then_inc(pv_done, 1)

            pe.wait_ge(ones_set, 1)
            for event, item in opening():
                if event == "piece":
                    form_piece(0, 0, item)
                elif event == "turn":
                    turn_rows(0, item, 1, 0)

            def body(n, u, first, last):
                for s in range(NS):
                    pieces = iter(shares(of_step(PIECES_AT, s, n, u, last), ORDER.count("piece")))
                    for item in ORDER:
                        if item == "piece":
                            for piece in next(pieces):
                                form_piece(*piece)
                        elif item == "pv":
                            if s:
                                pv(n, u, s - 1, rows_before(s, n, last), accs_before(s, n))
                            elif not first:
                                pv(n - 1, 1 - u, NS - 1, None, None)
                        else:
                            scores(n, u, s, item, first)
                    if at := ended(s, 2, n, first):
                        turn_acc(*at)
                    for unit, par, c in of_step(ROWS_AT, s, n, u, last):
                        turn_rows(unit, c, idle_bank(s), accs_before(s + 1, n))
                if last:
                    pv(n, u, NS - 1, None, None)
                    turn_acc(n, NCH - 1)

            over_units(pe, body)


def build_mlp(nc, io, keep, scr):
    with ExitStack() as ctx:
        t = Tensors(nc, ctx)
        o_in = [t.sb(f"o_in{i}", [P, TT, DIM]) for i in range(2)]
        x = [t.sb(f"mx{i}", [P, TT, DIM]) for i in range(2)]
        x1 = [t.sb(f"x1{i}", [P, TT, DIM]) for i in range(2)]
        xn = t.sb("mxn", [P, TT, DIM])
        o_t = t.sb("o_t", [P, 2, KD, CH], F32R)
        xn_t = t.sb("mxn_t", [P, 2, KD, CH], F32R)
        norm = Norm(t, "mlp")
        relu = t.sb("relu", [P, KH, CH])
        square = t.sb("square", [P, KH, CH])
        hid = t.sb("hid", [P, 2, KH, CH], F32R)
        y_sb = t.sb("y_sb", [P, TT, DIM])
        y = [t.sb(f"y{i}", [P, TT, DIM]) for i in range(2)]
        ps_h = t.ps("ps_h", [P, 2, CH])
        ps_t = t.ps("mps_t", [P, 2, CH])
        ps_o = t.ps("ps_o", [P, 2, 512])
        ps_y = t.ps("ps_y", [P, 2, 512])
        o_loaded, x_loaded = [t.sem(f"o_loaded{i}") for i in range(2)], [t.sem(f"x_loaded{i}") for i in range(2)]
        xb_done = t.sem("xb_done")
        turned, turned_copied, turned_split = t.sem("turned"), t.sem("turned_copied"), t.sem("turned_split")
        o_ready, x1_ready = t.sem("o_ready"), t.sem("x1_ready")
        xn_ready = t.sem("mxn_ready")
        hid_ready, relu_done, square_done = t.sem("hid_ready"), t.sem("relu_done"), t.sem("square_done")
        high_done, low_done = t.sem("high_done"), t.sem("low_done")
        y_ready, y_scaled, y_done, y_passed = t.sem("y_ready"), t.sem("y_scaled"), t.sem("y_done"), t.sem("y_passed")
        y_stored = [t.sem(f"y_stored{i}") for i in range(2)]
        block = ctx.enter_context(nc.Block())
        x_dram = io["x"].rearrange("b (c t p) d -> (b c) p t d", c=NCH, p=P)
        y_dram = io["out"].rearrange("b (c t p) d -> (b c) p t d", c=NCH, p=P)
        o_dram = scr["o"].rearrange("b c p t g e -> (b c) p (t g e)")
        uses = BATCH * NCH // 2

        def flat(tile, i):
            return tile[:, 2 * i:2 * i + 2].rearrange("p t d -> p (t d)")

        @block.sync
        def _(sp):
            def load(n, u):
                sp.dma_start(o_in[u][:].rearrange("p t d -> p (t d)"), o_dram[bass.ts(n, 1)].rearrange("o p e -> (o p) e")
                             ).then_inc(o_loaded[u], 16)
                sp.dma_start(x[u][:], x_dram[bass.ts(n, 1)].rearrange("o p t d -> (o p) t d")).then_inc(x_loaded[u], 16)

            load(0, 0)
            load(1, 1)

            def body(n, used, u, left):
                if left >= 2:
                    sp.wait_ge(x1_ready, 2 * (n + 1))
                    load(n + 2, u)
                if isinstance(n, int):
                    sp.wait_ge(y_done, 2 * (n + 1))
                else:
                    wait_apart(sp, y_done, 2 * (n + 1), y_passed)
                sp.dma_start(y_dram[bass.ts(n, 1)].rearrange("o p t d -> (o p) t d"), y[u][:]).then_inc(y_stored[u], 16)

            over_chunks(sp, body)
            for i in range(2):
                sp.wait_ge(y_stored[i], 16 * uses)

        @block.gpsimd
        def _(pool):
            def add_bias(n, used, u):
                pool.wait_ge(x_loaded[u], 16 * (used + 1))
                for tt in range(TT):
                    last = pool.tensor_tensor(x[u][:, tt], x[u][:, tt], keep["b_o"][:], ALU.add)
                last.then_inc(xb_done, 1)

            add_bias(0, 0, 0)

            def body(n, used, u, left):
                if left >= 1:
                    add_bias(n + 1, used + u, 1 - u)
                for m in range(KH):
                    pool.wait_ge(high_done, KH * n + m + 1)
                    pool.tensor_tensor(hid[:, 1, m], square[:, m], hid[:, 0, m].bitcast(F32), ALU.subtract).then_inc(low_done, 1)

            over_chunks(pool, body)

        @block.vector
        def _(dve):
            def residual_norm(n, u):
                dve.wait_ge(xb_done, n + 1)
                for i in range(2):
                    dve.wait_ge(o_ready, 2 * n + i + 1)
                    dve.tensor_tensor(flat(x1[u], i), ps_o[:, i], flat(x[u], i), ALU.add).then_inc(x1_ready, 1)
                dve.wait_ge(x1_ready, 2 * (n + 1))
                norm.normalise(dve, x1[u], xn, n).then_inc(xn_ready, 1)

            copy_low(dve, o_t, ps_t, turned_copied, turned_split, 0)
            residual_norm(0, 0)
            copy_low(dve, xn_t, ps_t, turned_copied, turned_split, 2)

            def body(n, used, u, left):
                for m in range(KH):
                    dve.wait_ge(relu_done, KH * n + m + 1)
                    if not zero(n):
                        dve.wait_ge(low_done, KH * (n - 1) + m + 1)
                    dve.tensor_tensor(square[:, m], relu[:, m], relu[:, m], ALU.mult).then_inc(square_done, 1)
                    dve.wait_ge(square_done, KH * n + m + 1)
                    dve.tensor_copy(hid[:, 0, m], square[:, m]).then_inc(high_done, 1)
                    if m == 4 and left >= 1:
                        copy_low(dve, o_t, ps_t, turned_copied, turned_split, 4 * (n + 1))
                if left >= 1:
                    if not zero(n):
                        dve.wait_ge(y_done, 2 * n)
                    residual_norm(n + 1, 1 - u)
                if not zero(used):
                    dve.wait_ge(y_stored[u], 16 * used)
                for i in range(2):
                    dve.wait_ge(y_ready, 2 * n + i + 1)
                    dve.tensor_tensor(y_sb[:, 2 * i:2 * i + 2], ps_y[:, i].rearrange("p (t d) -> p t d", d=DIM),
                                      keep["s_out"][:].rearrange("p (o d) -> p o d", o=1).to_broadcast([P, 2, DIM]),
                                      ALU.mult).then_inc(y_scaled, 1)
                    dve.wait_ge(y_scaled, 2 * n + i + 1)
                    dve.tensor_tensor(flat(y[u], i), flat(y_sb, i), flat(x1[u], i), ALU.add).then_inc(y_done, 1)
                    if i == 0 and left >= 1:
                        copy_low(dve, xn_t, ps_t, turned_copied, turned_split, 4 * (n + 1) + 2)

            over_chunks(dve, body)

        @block.scalar
        def _(act):
            copy_high(act, o_t, ps_t, turned, turned_copied, 0)
            norm.take_root(act, 0)

            def body(n, used, u, left):
                copy_high(act, xn_t, ps_t, turned, turned_copied, 4 * n + 2)
                for m in range(KH):
                    act.wait_ge(hid_ready, KH * n + m + 1)
                    if not zero(n):
                        act.wait_ge(square_done, KH * (n - 1) + m + 1)
                    act.activation(relu[:, m], ps_h[:, m % 2], ACT.Relu).then_inc(relu_done, 1)
                    if m == 3 and left >= 1:
                        copy_high(act, o_t, ps_t, turned, turned_copied, 4 * (n + 1))
                if left >= 1:
                    norm.take_root(act, n + 1)

            over_chunks(act, body)

        @block.tensor
        def _(pe):
            def turn(src, first):
                if not zero(first):
                    pe.wait_ge(turned_split, first)
                for k in range(KD):
                    for tt in range(TT):
                        last = pe.transpose(ps_t[:, k, tt * P:(tt + 1) * P], src[:, tt, k * P:(k + 1) * P], keep["ident"][:])
                    last.then_inc(turned, 1)

            def turn_o(n, used, u):
                pe.wait_ge(o_loaded[u], 16 * (used + 1))
                turn(o_in[u], 4 * n)

            def project(n):
                pe.wait_ge(turned_split, 4 * n + 2)
                if not zero(n):
                    pe.wait_ge(x1_ready, 2 * n)
                for tt in range(TT):
                    for k in range(KD):
                        last = split_products(pe, ps_o[:, tt // 2, (tt % 2) * DIM:(tt % 2 + 1) * DIM],
                                              [o_t[:, a, k, tt * P:(tt + 1) * P] for a in range(2)],
                                              [keep["w_o"][:, a, k] for a in range(2)], k == 0, k == KD - 1)
                    if tt % 2:
                        last.then_inc(o_ready, 1)

            def turn_xn(n):
                pe.wait_ge(xn_ready, n + 1)
                turn(xn, 4 * n + 2)

            turn_o(0, 0, 0)
            project(0)
            turn_xn(0)

            def body(n, used, u, left):
                pe.wait_ge(turned_split, 4 * n + 4)
                for m in range(KH):
                    if m >= 2:
                        pe.wait_ge(relu_done, KH * n + m - 1)
                    for k in range(KD):
                        last = split_products(pe, ps_h[:, m % 2], [keep["w1"][:, a, k, m * P:(m + 1) * P] for a in range(2)],
                                              [xn_t[:, a, k] for a in range(2)], k == 0, k == KD - 1)
                    last.then_inc(hid_ready, 1)
                    if m == 1 and left >= 1:
                        turn_o(n + 1, used + u, 1 - u)
                if left >= 1:
                    project(n + 1)
                if not zero(n):
                    pe.wait_ge(y_scaled, 2 * n)
                for i in range(2):
                    for m in range(KH):
                        if i == 0:
                            pe.wait_ge(low_done, KH * n + m + 1)
                        for tt in (2 * i, 2 * i + 1):
                            for a in range(2):
                                last = pe.matmul(ps_y[:, i, (tt % 2) * DIM:(tt % 2 + 1) * DIM], hid[:, a, m, tt * P:(tt + 1) * P],
                                                 keep["w2"][:, m], start=(m == 0 and a == 0 and tt % 2 == 0),
                                                 stop=(m == KH - 1 and a == 1), skip_group_check=True)
                        if (i, m) == (1, KH // 2 - 1) and left >= 1:
                            turn_xn(n + 1)
                    last.then_inc(y_ready, 1)

            over_chunks(pe, body)


def build_layer(nc, io):
    with ExitStack() as ctx:
        t = Tensors(nc, ctx)
        keep = {
            "w_qkv": t.sb("w_qkv", [P, 2, KD, 3 * DIM], F32R),
            "w_o": t.sb("w_o", [P, 2, KD, DIM], F32R),
            "w1": t.sb("w1", [P, 2, KD, HID], F32R),
            "w2": t.sb("w2", [P, KH, DIM], F32R),
            "s_out": t.sb("s_out", [P, DIM]),
            "b_qk": t.sb("b_qk", [P, 2 * KD]),
            "b_qs": t.sb("b_qs", [P, KD]),
            "b_v": t.sb("b_v", [P, DIM]),
            "b_o": t.sb("b_o", [P, DIM]),
            "ident": t.sb("ident", [P, P]),
            "ident_h": t.sb("ident_h", [P, P], BF16),
            "mask_qk": t.sb("mask_qk", [P, CH]),
        }
        scr = {
            "q": nc.dram_tensor("q_scr", [BATCH, PARTS, DIM, SEQ], BF16).ap(),
            "k": nc.dram_tensor("k_scr", [BATCH, PARTS, DIM, SEQ], BF16).ap(),
            "v": nc.dram_tensor("v_scr", [BATCH, P, KT, GROUPS, GH * VW], F32).ap(),
            "o": nc.dram_tensor("o_scr", [BATCH, NCH, P, TT, GROUPS, GH * HD], F32).ap(),
        }
        build_prep(nc, io, keep)
        build_qkv(nc, io, keep, scr)
        build_attention(nc, io, keep, scr)
        build_mlp(nc, io, keep, scr)


_INS = {
    "L0_attn_x": "x", "L0_attn_W_attn": "W_attn", "L0_attn_b_attn": "b_attn", "L0_attn_W_proj": "W_proj",
    "L0_attn_b_proj": "b_proj", "L0_ffn_fast_b": "fast_b", "L0_ffn_w_fc": "w_fc", "L0_ffn_w_proj": "w_proj",
    "L0_ffn_u": "u", "L0_ffn_v": "v", "L0_ffn_gate": "gate",
}


def kernel(**inputs):
    import numpy as _np
    import concourse.bacc as _bacc
    from concourse import mybir as _mybir
    from concourse.bass_utils import run_bass_kernel_spmd as _run

    nc = _bacc.Bacc("TRN2", target_bir_lowering=False, num_devices=1)
    arrays, io = {}, {}
    for name, short in _INS.items():
        a = _np.ascontiguousarray(inputs[name])
        a = a.reshape(a.shape or (1,))
        arrays[f"in_{name}"] = a
        io[short] = nc.dram_tensor(f"in_{name}", a.shape, _mybir.dt.from_np(a.dtype), kind="ExternalInput").ap()
    io["out"] = nc.dram_tensor("out", (BATCH, SEQ, DIM), F32, kind="ExternalOutput").ap()
    build_layer(nc, io)
    r = _run(nc, [arrays], core_ids=[0])
    return r.results[0]["out"]
```
